# Optimizing a Trainium2 kernel written in Bass

```python
import numpy as np
import jax
import jax.numpy as jnp

def _softmax(x, axis=-1):
    return jax.nn.softmax(x, axis=axis)

def _gelu(x):
    return jax.nn.gelu(x, approximate=True)

def _silu(x):
    return jax.nn.silu(x)

def _sigmoid(x):
    return jax.nn.sigmoid(x)

def _layernorm(x, axis=-1, eps=1e-05):
    m = jnp.mean(x, axis=axis, keepdims=True)
    v = jnp.var(x, axis=axis, keepdims=True)
    return (x - m) / jnp.sqrt(v + eps)

def _scatter_add(tgt, idx, src, axis=0):
    return tgt.at[idx].add(src)

def _segment_sum(src, seg, n):
    return jax.ops.segment_sum(src, seg, n)
kernel_name = 'mk_seq_postln_d2_jaxref_r4_4da8d8'

def setup_inputs(seed: int=0):
    np.random.seed(seed)
    _w = jnp.asarray

    def _L0_attn_setup():
        import jax, jax.numpy as jnp
        import numpy as np
        B, T, D = (4, 512, 256)
        H, DK = (8, 64)
        EPS = 1e-06

        def _xavier(key, shape):
            fan_in, fan_out = (shape[1], shape[0])
            lim = float(np.sqrt(6.0 / (fan_in + fan_out)))
            return jax.random.uniform(key, shape, jnp.float32, -lim, lim)

        def _phi(u):
            return jax.nn.elu(u) + 1.0
        key = jax.random.key(seed)
        ks = jax.random.split(key, 7)
        x = jax.random.normal(ks[0], (B, T, D), jnp.float32)
        W_Q = _xavier(ks[1], (H * DK, D))
        W_K = _xavier(ks[2], (H * DK, D))
        W_V = _xavier(ks[3], (H * DK, D))
        W_g_w = _xavier(ks[4], (H * DK, D))
        W_g_b = jax.random.normal(ks[5], (H * DK,), jnp.float32) * 0.02
        W_O = _xavier(ks[6], (D, H * DK))
        decay_log = jnp.zeros((H,), jnp.float32)
        return {'x': x, 'W_Q': W_Q, 'W_K': W_K, 'W_V': W_V, 'W_g_w': W_g_w, 'W_g_b': W_g_b, 'W_O': W_O, 'decay_log': decay_log}
    _L0_attn_in = _L0_attn_setup()

    def _L0_ffn_setup():
        import jax, jax.numpy as jnp
        import numpy as np
        DIM = 256

        def _reference_tuple_inner(x, W_r, W_k, W_v, mu_r, mu_k):
            B, T, C = x.shape
            x_prev = jnp.concatenate([jnp.zeros((B, 1, C), x.dtype), x[:, :-1, :]], axis=1)
            xr = mu_r * x + (1.0 - mu_r) * x_prev
            xk = mu_k * x + (1.0 - mu_k) * x_prev
            r = jax.nn.sigmoid(jnp.einsum('btc,dc->btd', xr, W_r))
            k = jnp.einsum('btc,dc->btd', xk, W_k)
            k_act = jnp.square(jax.nn.relu(k))
            out = r * jnp.einsum('btc,dc->btd', k_act, W_v)
            new_state = x[:, -1, :]
            return (out, new_state)
        key = jax.random.key(seed)
        ks = jax.random.split(key, 6)
        B, T, C = (8, 512, DIM)
        x = jax.random.normal(ks[0], (B, T, C), dtype=jnp.float32)
        s = 1.0 / np.sqrt(C)
        W_r = jax.random.uniform(ks[1], (C, C), jnp.float32, -s, s)
        W_k = jax.random.uniform(ks[2], (C, C), jnp.float32, -s, s)
        W_v = jax.random.uniform(ks[3], (C, C), jnp.float32, -s, s)
        mu_r = jax.random.uniform(ks[4], (C,), jnp.float32)
        mu_k = jax.random.uniform(ks[5], (C,), jnp.float32)
        return {'x': x, 'W_r': W_r, 'W_k': W_k, 'W_v': W_v, 'mu_r': mu_r, 'mu_k': mu_k}
    _L0_ffn_in = _L0_ffn_setup()

    def _L1_attn_setup():
        import jax, jax.numpy as jnp
        import numpy as np
        HIDDEN = 256
        NUM_HEADS = 16
        NUM_KV = 4
        HEAD_DIM = HIDDEN // NUM_HEADS
        GROUPS = NUM_HEADS // NUM_KV
        SCALE = HEAD_DIM ** 0.5
        key = jax.random.key(seed)
        ks = jax.random.split(key, 9)
        s = 0.02
        B, N = (4, 512)
        return {'x': jax.random.normal(ks[0], (B, N, HIDDEN), dtype=jnp.float32), 'Wq': jax.random.normal(ks[1], (HIDDEN, NUM_HEADS * HEAD_DIM), dtype=jnp.float32) * s, 'bq': jnp.zeros((NUM_HEADS * HEAD_DIM,), dtype=jnp.float32), 'Wk': jax.random.normal(ks[2], (HIDDEN, NUM_KV * HEAD_DIM), dtype=jnp.float32) * s, 'bk': jnp.zeros((NUM_KV * HEAD_DIM,), dtype=jnp.float32), 'Wv': jax.random.normal(ks[3], (HIDDEN, NUM_KV * HEAD_DIM), dtype=jnp.float32) * s, 'bv': jnp.zeros((NUM_KV * HEAD_DIM,), dtype=jnp.float32), 'Wo': jax.random.normal(ks[4], (NUM_HEADS * HEAD_DIM, HIDDEN), dtype=jnp.float32) * s, 'bo': jnp.zeros((HIDDEN,), dtype=jnp.float32)}
    _L1_attn_in = _L1_attn_setup()

    def _L1_ffn_setup():
        import jax, jax.numpy as jnp
        import numpy as np
        B, S, D_MODEL, D_FF = (4, 512, 256, 1024)

        def _quantum_transform(hidden, theta, w_real, w_imag):
            imag = w_imag * jnp.sin(theta + hidden * 0.1)
            quantum_phase = jnp.cos(theta) * w_real + jnp.sin(theta) * w_imag
            return hidden + quantum_phase * imag * 0.1
        key = jax.random.key(seed)
        ks = jax.random.split(key, 8)
        return {'x': jax.random.normal(ks[0], (B, S, D_MODEL), dtype=jnp.float32), 'W1': jax.random.normal(ks[1], (D_MODEL, D_FF), dtype=jnp.float32) * (1.0 / np.sqrt(D_MODEL)), 'b1': jnp.zeros((D_FF,), dtype=jnp.float32), 'quantum_phases': jax.random.normal(ks[2], (D_FF,), dtype=jnp.float32) * (2.0 * np.pi), 'quantum_weights_real': jax.random.normal(ks[3], (D_FF,), dtype=jnp.float32) * 0.1, 'quantum_weights_imag': jax.random.normal(ks[4], (D_FF,), dtype=jnp.float32) * 0.1, 'W2': jax.random.normal(ks[5], (D_FF, D_MODEL), dtype=jnp.float32) * (1.0 / np.sqrt(D_FF)), 'b2': jnp.zeros((D_MODEL,), dtype=jnp.float32)}
    _L1_ffn_in = _L1_ffn_setup()
    _d = {'L0_attn_x': _L0_attn_in['x'], 'L0_attn_W_Q': _L0_attn_in['W_Q'], 'L0_attn_W_K': _L0_attn_in['W_K'], 'L0_attn_W_V': _L0_attn_in['W_V'], 'L0_attn_W_g_w': _L0_attn_in['W_g_w'], 'L0_attn_W_g_b': _L0_attn_in['W_g_b'], 'L0_attn_W_O': _L0_attn_in['W_O'], 'L0_attn_decay_log': _L0_attn_in['decay_log'], 'L0_ffn_W_r': _L0_ffn_in['W_r'], 'L0_ffn_W_k': _L0_ffn_in['W_k'], 'L0_ffn_W_v': _L0_ffn_in['W_v'], 'L0_ffn_mu_r': _L0_ffn_in['mu_r'], 'L0_ffn_mu_k': _L0_ffn_in['mu_k'], 'L1_attn_Wq': _L1_attn_in['Wq'], 'L1_attn_bq': _L1_attn_in['bq'], 'L1_attn_Wk': _L1_attn_in['Wk'], 'L1_attn_bk': _L1_attn_in['bk'], 'L1_attn_Wv': _L1_attn_in['Wv'], 'L1_attn_bv': _L1_attn_in['bv'], 'L1_attn_Wo': _L1_attn_in['Wo'], 'L1_attn_bo': _L1_attn_in['bo'], 'L1_ffn_W1': _L1_ffn_in['W1'], 'L1_ffn_b1': _L1_ffn_in['b1'], 'L1_ffn_quantum_phases': _L1_ffn_in['quantum_phases'], 'L1_ffn_quantum_weights_real': _L1_ffn_in['quantum_weights_real'], 'L1_ffn_quantum_weights_imag': _L1_ffn_in['quantum_weights_imag'], 'L1_ffn_W2': _L1_ffn_in['W2'], 'L1_ffn_b2': _L1_ffn_in['b2']}
    _x0 = _d['L0_attn_x']
    _d['L0_attn_x'] = jax.random.normal(jax.random.fold_in(jax.random.key(seed), 1), (16, 1024, 256), dtype=_x0.dtype)
    del _x0
    return _d

def reference(L0_attn_x, L0_attn_W_Q, L0_attn_W_K, L0_attn_W_V, L0_attn_W_g_w, L0_attn_W_g_b, L0_attn_W_O, L0_attn_decay_log, L0_ffn_W_r, L0_ffn_W_k, L0_ffn_W_v, L0_ffn_mu_r, L0_ffn_mu_k, L1_attn_Wq, L1_attn_bq, L1_attn_Wk, L1_attn_bk, L1_attn_Wv, L1_attn_bv, L1_attn_Wo, L1_attn_bo, L1_ffn_W1, L1_ffn_b1, L1_ffn_quantum_phases, L1_ffn_quantum_weights_real, L1_ffn_quantum_weights_imag, L1_ffn_W2, L1_ffn_b2):

    def _L0_attn_ref(x, W_Q, W_K, W_V, W_g_w, W_g_b, W_O, decay_log):
        import jax, jax.numpy as jnp
        import numpy as np
        B, T, D = (4, 512, 256)
        H, DK = (8, 64)
        EPS = 1e-06

        def _xavier(key, shape):
            fan_in, fan_out = (shape[1], shape[0])
            lim = float(np.sqrt(6.0 / (fan_in + fan_out)))
            return jax.random.uniform(key, shape, jnp.float32, -lim, lim)

        def _phi(u):
            return jax.nn.elu(u) + 1.0
        b, t, d = x.shape
        q = _phi((x @ W_Q.T).reshape(b, t, H, DK))
        k = _phi((x @ W_K.T).reshape(b, t, H, DK))
        v = (x @ W_V.T).reshape(b, t, H, DK)
        gamma = jax.nn.sigmoid(decay_log)
        g4 = gamma[None, :, None, None]
        g3 = gamma[None, :, None]
        qT = jnp.moveaxis(q, 1, 0)
        kT = jnp.moveaxis(k, 1, 0)
        vT = jnp.moveaxis(v, 1, 0)
        S0 = jnp.zeros((b, H, DK, DK), x.dtype)
        z0 = jnp.zeros((b, H, DK), x.dtype)

        def step(carry, inp):
            S, z = carry
            qt, kt, vt = inp
            S = g4 * S + jnp.einsum('bhi,bhj->bhij', kt, vt)
            z = g3 * z + kt
            num = jnp.einsum('bhij,bhi->bhj', S, qt)
            den = jnp.sum(z * qt, axis=-1, keepdims=True) + EPS
            return ((S, z), num / den)
        _, ys = jax.lax.scan(step, (S0, z0), (qT, kT, vT))
        outputs = jnp.moveaxis(ys, 0, 1)
        gate = jax.nn.sigmoid(x @ W_g_w.T + W_g_b).reshape(b, t, H, DK)
        y = (outputs * gate).reshape(b, t, H * DK)
        return y @ W_O.T

    def _L0_ffn_ref(x, W_r, W_k, W_v, mu_r, mu_k):
        import jax, jax.numpy as jnp
        import numpy as np
        DIM = 256

        def _reference_tuple_inner(x, W_r, W_k, W_v, mu_r, mu_k):
            B, T, C = x.shape
            x_prev = jnp.concatenate([jnp.zeros((B, 1, C), x.dtype), x[:, :-1, :]], axis=1)
            xr = mu_r * x + (1.0 - mu_r) * x_prev
            xk = mu_k * x + (1.0 - mu_k) * x_prev
            r = jax.nn.sigmoid(jnp.einsum('btc,dc->btd', xr, W_r))
            k = jnp.einsum('btc,dc->btd', xk, W_k)
            k_act = jnp.square(jax.nn.relu(k))
            out = r * jnp.einsum('btc,dc->btd', k_act, W_v)
            new_state = x[:, -1, :]
            return (out, new_state)
        return _reference_tuple_inner(x, W_r, W_k, W_v, mu_r, mu_k)[0]

    def _L1_attn_ref(x, Wq, bq, Wk, bk, Wv, bv, Wo, bo):
        import jax, jax.numpy as jnp
        import numpy as np
        HIDDEN = 256
        NUM_HEADS = 16
        NUM_KV = 4
        HEAD_DIM = HIDDEN // NUM_HEADS
        GROUPS = NUM_HEADS // NUM_KV
        SCALE = HEAD_DIM ** 0.5
        B, N, _ = x.shape
        q = x @ Wq + bq
        k = x @ Wk + bk
        v = x @ Wv + bv
        q = q.reshape(B, N, NUM_HEADS, HEAD_DIM).transpose(0, 2, 1, 3)
        q = q.reshape(B, NUM_KV, GROUPS, N, HEAD_DIM).transpose(0, 2, 1, 3, 4)
        k = k.reshape(B, N, NUM_KV, HEAD_DIM).transpose(0, 2, 1, 3)
        v = v.reshape(B, N, NUM_KV, HEAD_DIM).transpose(0, 2, 1, 3)
        scores = jnp.einsum('bghnd,bhsd->bghns', q, k)
        attn = jax.nn.softmax(scores / SCALE, axis=-1)
        out = jnp.einsum('bghns,bhsd->bghnd', attn, v)
        out = out.transpose(0, 3, 1, 2, 4).reshape(B, N, NUM_HEADS * HEAD_DIM)
        return out @ Wo + bo

    def _L1_ffn_ref(x, W1, b1, quantum_phases, quantum_weights_real, quantum_weights_imag, W2, b2):
        import jax, jax.numpy as jnp
        import numpy as np
        B, S, D_MODEL, D_FF = (4, 512, 256, 1024)

        def _quantum_transform(hidden, theta, w_real, w_imag):
            imag = w_imag * jnp.sin(theta + hidden * 0.1)
            quantum_phase = jnp.cos(theta) * w_real + jnp.sin(theta) * w_imag
            return hidden + quantum_phase * imag * 0.1
        hidden = jnp.einsum('bsd,df->bsf', x, W1) + b1
        q = _quantum_transform(hidden, quantum_phases, quantum_weights_real, quantum_weights_imag)
        act = jax.nn.relu(q)
        return jnp.einsum('bsf,fd->bsd', act, W2) + b2
    x = L0_attn_x
    x = _layernorm(x + _L0_attn_ref(x, L0_attn_W_Q, L0_attn_W_K, L0_attn_W_V, L0_attn_W_g_w, L0_attn_W_g_b, L0_attn_W_O, L0_attn_decay_log), axis=-1)
    x = _layernorm(x + _L0_ffn_ref(x, L0_ffn_W_r, L0_ffn_W_k, L0_ffn_W_v, L0_ffn_mu_r, L0_ffn_mu_k), axis=-1)
    x = _layernorm(x + _L1_attn_ref(x, L1_attn_Wq, L1_attn_bq, L1_attn_Wk, L1_attn_bk, L1_attn_Wv, L1_attn_bv, L1_attn_Wo, L1_attn_bo), axis=-1)
    x = _layernorm(x + _L1_ffn_ref(x, L1_ffn_W1, L1_ffn_b1, L1_ffn_quantum_phases, L1_ffn_quantum_weights_real, L1_ffn_quantum_weights_imag, L1_ffn_W2, L1_ffn_b2), axis=-1)
    return x

_drawn_inputs = setup_inputs


def setup_inputs(seed=0):
    import zlib

    import numpy as np

    out = dict(_drawn_inputs(seed))
    spreads = {'L0_attn_decay_log': (0.0, 0.8),
     'L1_attn_bq': (0.0, 0.8),
     'L1_attn_bk': (0.0, 2.0),
     'L1_attn_bv': (0.0, 0.286),
     'L1_attn_bo': (0.0, 0.1),
     'L1_ffn_b1': (0.0, 0.1),
     'L1_ffn_b2': (0.0, 0.1)}
    factors = {'L0_attn_W_Q': 6.817,
     'L0_attn_W_K': 3.438,
     'L0_attn_W_g_b': 8.0,
     'L0_ffn_W_r': 3.137,
     'L0_ffn_mu_r': 6.476,
     'L1_attn_Wq': 8.0,
     'L1_attn_Wk': 8.0,
     'L1_attn_Wv': 8.0,
     'L1_ffn_quantum_phases': 8.0,
     'L1_ffn_quantum_weights_real': 35.694,
     'L1_ffn_quantum_weights_imag': 8.0}
    for name, (base, spread) in spreads.items():
        noise = np.random.default_rng([zlib.crc32(name.encode()), seed]).standard_normal(out[name].shape)
        drawn = base * np.exp(spread * noise) if base else spread * noise
        out[name] = jnp.asarray(drawn.astype(out[name].dtype))
    for name, factor in factors.items():
        out[name] = (out[name] * factor).astype(out[name].dtype)
    return out
```

```python
from contextlib import ExitStack

import numpy as np

import concourse.bass as bass
from concourse import mybir

F32 = mybir.dt.float32
BF16 = mybir.dt.bfloat16
ACT = mybir.ActivationFunctionType
ALU = mybir.AluOpType
AX = mybir.AxisListType

P = 128
T = 1024
D = 256
KD = D // P
HALF = 512
TT = HALF // P
NT = T // P
H0, DK = 8, 64
NP0 = H0 * DK // P
WIN = DK + 1
KV, GR, HD = 4, 4, 16
NF = 1024 // P
KSTACK = 99
LN_EPS = 1e-5
DEN_EPS = 1e-6
MAGIC = 12582912.0
TWO_PI = 6.283185307179586
TURN = 6.2831850
PI_A, PI_B = 6.28125, 0.0019350051879882812
PI_C = TWO_PI - PI_A - PI_B


def batch_order():
    o = []

    def project(h):
        o.extend(("xt", h, k) for k in range(KD))
        o.extend(("g", h, t) for t in range(TT))
        if h == 1:
            o.extend([("yt", 0, 3), ("w", 0, 3), ("nb", 0, 2)])
        o.extend(("v", h, t) for t in range(TT))
        if h == 1:
            o.append(("nb", 0, 3))
        for p in range(NP0):
            o.extend([("q", h, p), ("k", h, p)])
            if p:
                o.append(("kn", h, p - 1))
        o.append(("kn", h, NP0 - 1))

    def recur(h):
        steps = [(c, pp) for c in range(TT) for pp in range(2)]
        o.append(("a", h, *steps[0]))
        for n, (c, pp) in enumerate(steps):
            if n + 1 < len(steps):
                o.append(("a", h, *steps[n + 1]))
            if (h, c) != (1, TT - 1):
                o.append(("u", h, c, pp))
            o.append(("o", h, c, pp))
            if pp == 1 and c >= 1:
                o.extend([("yt", h, c - 1), ("w", h, c - 1)])
                if c >= 2:
                    o.append(("nb", 0, h * TT + c - 2))

    o.append(("init",))
    project(0)
    recur(0)
    project(1)
    recur(1)
    o.extend([("yt", 1, 3), ("w", 1, 3), ("nb", 0, 6)])
    for h in range(2):
        if h == 1:
            o.append(("nb", 1, 3))
        o.extend(("x1", h, k) for k in range(KD))
        o.append(("mix", h))
        if h == 0:
            o.append(("nb", 0, 7))
        o.extend(("kf", h, m) for m in range(KD))
        for t in range(TT):
            o.append(("rv", h, t))
            if t:
                o.append(("nb", 1, h * TT + t - 1))
    for h in range(2):
        if h == 1:
            pass
        o.extend(("x2", h, k) for k in range(KD))
        if h == 0:
            o.append(("nb", 1, 7))
        o.extend(("pq", h, m) for m in range(KD))
        o.extend([("pk", h), ("pv", h)])
        o.append(("bo", h))
    o.append(("stack",))
    o.extend(("mx", 0, n) for n in range(GR * NT))
    o.append(("mt", 0))
    for g in range(KV):
        ahead = [("mx", g + 1, n) for n in range(GR * NT)] if g + 1 < KV else []
        for c in range(NT):
            if c == NT - 1 and g + 1 < KV:
                o.append(("mt", g + 1))
            for h in range(GR):
                o.append(("s", g, c, h))
                left = (NT - 1) * GR - (c * GR + h)
                for _ in range(-(-len(ahead) // left) if c and left > 0 else 0):
                    o.append(ahead.pop(0))
            if c:
                o.append(("av", g, c - 1))
            if c == 2 and g:
                o.append(("on", g - 1))
        o.extend([("av", g, NT - 1), ("ot", g)])
    o.append(("on", KV - 1))
    for t in range(NT):
        o.append(("wo", t))
        if t:
            o.append(("nb", 2, t - 1))
    o.extend(("x3", 0, k) for k in range(KD))
    o.append(("nb", 2, 7))
    for f in range(NF):
        o.append(("h", 0, f))
    o.extend(("x3", 1, k) for k in range(KD))
    o.append(("hb", 0, NF - 1))
    o.append(("b2",))
    for f in range(NF):
        o.append(("h", 1, f))
        if f % 2:
            t = f // 2
            o.append(("w2", 0, t))
            if t:
                o.append(("nb", 3, t - 1))
    o.append(("hb", 1, NF - 1))
    o.append(("nb", 3, 3))
    o.append(("out", 0))
    for t in range(TT):
        o.append(("w2", 1, t))
        if t:
            o.append(("nb", 3, TT + t - 1))
    o.extend([("nb", 3, 7), ("out", 1)])
    return o


RING = ("xt", "g", "v", "q", "k", "kn", "yt", "w", "x1", "kf", "rv", "x2", "pq", "pk", "pv", "wo", "x3", "h", "w2")


def plan_banks(order):
    uses = [0] * 8
    plan = {}
    last = {}
    for turn in range(2):
        uses = [0] * 8
        n = 0
        for key in order:
            k = key[0]
            if k == "a":
                subs = [(key[:3] + (2 * key[3] + j,), [4 + j]) for j in range(2)]
            elif k == "u":
                subs = [(key[:3] + (2 * key[3] + j,), [(n + j) % 4]) for j in range(2)]
                n += 2
            elif k == "o":
                subs = [(key, [6 + key[3]])]
            elif k == "mx":
                subs = [(key + (j,), [4 + j]) for j in range(2)]
            elif k == "mt":
                subs = [(key, [4])]
            elif k == "s":
                subs = [(key, [0, 1] if key[3] % 2 == 0 else [2, 3])]
            elif k == "av":
                subs = [(("ot", key[1]), [6, 7])] if key[2] == 0 else []
            elif k in RING:
                subs = [(key, [n % 4])]
                n += 1
            else:
                subs = []
            for sub, banks in subs:
                before = {last[x] for x in banks if x in last}
                plan[sub] = (banks, before, uses[banks[0]])
                for x in banks:
                    last[x] = (sub, turn)
                uses[banks[0]] += 1
    return plan, uses


def program(nc, A, out):
    NB = A["x"].shape[0]
    order = batch_order()
    plan, uses = plan_banks(order)
    ctx = ExitStack()
    with ctx:
        def sb(name, shape, dt=F32):
            return ctx.enter_context(nc.sbuf_tensor(name, shape, dt))

        per = {
            "x_in": 16, "init": 2, "xt": 4, "gz": 8, "gate": 8, "vz": 8,
            "neg": 16, "er": 16, "phi": 16, "qs": 8, "kn": 8, "am": 32, "state": 28, "o_step": 32, "o_div": 16, "y": 16,
            "yt": 8, "ln_step": 64, "ln_stat": 32, "ln_eps": 32, "ln_rstd": 32, "ln_done": 32,
            "x1": 4, "mix_tmp": 8, "mix": 8, "kr": 4, "ka": 4, "sg": 8, "rv_mul": 8,
            "x2": 4, "part1": 6, "rest1": 6, "part2": 6, "parts": 6, "v1": 2, "bo": 2,
            "ks": 16 * 6, "k_out": 16, "q_out": 16, "r_out": 16 * KV, "qs0": 16 * 12, "qs1": 16 * 12, "m0": 16 * 6, "m1": 16 * 6, "mx": 2 * KV * GR * NT, "nm": KV, "mt1": KV, "mt_r": KV, "mt2": KV, "m_parts": KV,
            "p": KV * NT * GR, "o_copy": KV, "sums": 16 * KV, "recip": KV, "r_in": 16 * KV * GR, "on": KV,
            "x3": 4, "fw": 16, "fn": 16, "fr": 16, "sin": 16, "fz": 16, "act": 16, "b2": 2, "out": 32,
        }
        S = {n: ctx.enter_context(nc.semaphore(n)) for n in per}
        filled = [ctx.enter_context(nc.semaphore(f"filled{b}")) for b in range(8)]
        loads = ctx.enter_context(nc.semaphore("constants_loaded"))
        c_pool = ctx.enter_context(nc.semaphore("c_pool"))
        c_act = ctx.enter_context(nc.semaphore("c_act"))
        c_dve = ctx.enter_context(nc.semaphore("c_dve"))

        START = {"ln_step": per["ln_step"], "out": per["out"]}

        def at(b, name, n):
            return b * per[name] + START.get(name, 0) + n

        w_in = sb("w_in", [P, 4, KD, H0 * DK])
        w_out = sb("w_out", [P, NP0, D])
        w_ffn = sb("w_ffn", [P, 3, KD, D])
        w_q1 = sb("w_q1", [P, KD, D])
        w_vk1 = sb("w_vk1", [P, KD, 2 * KV * HD])
        w_o1 = sb("w_o1", [P, KV, D])
        w_f1 = sb("w_f1", [P, KD, NF * P])
        w_f2 = sb("w_f2", [P, NF, D])
        ident = sb("ident", [P, P])
        decay = sb("decay", [P, H0, P])
        q_pow = sb("q_pow", [P, NP0, P])
        k_pow = sb("k_pow", [P, H0])
        c_pow = sb("c_pow", [P, NP0])
        gate_bias = sb("gate_bias", [P, H0 * DK])
        bo_row = sb("bo_row", [P, D])
        b2_row = sb("b2_row", [P, D])
        bv_row = sb("bv_row", [P, KV * HD])
        cols = sb("cols", [P, 64])
        bq, bk = cols[:, 0:2], cols[0:64, 2:3]
        mu, om = cols[:, 4:8], cols[:, 8:12]
        f_b1, f_turn, f_coef = cols[:, 16:24], cols[:, 24:32], cols[:, 32:40]
        minus_half, ln_eps = cols[:, 40:41], cols[:, 41:42]
        lg_pair = cols[:, 44:48]
        lg = cols[:, 48:56]

        x_in = sb("x_in", [P, NT, D])
        xn = sb("xn", [P, NT, D])
        r_a = sb("r_a", [P, KD, T + 1])
        x1T, x3T = r_a, r_a
        r_b = sb("r_b", [P, KD * T])
        x0T = r_b[:, 0:KD * HALF].rearrange("p (k n) -> p k n", k=KD)
        x2T = r_b[:, :].rearrange("p (k n) -> p k n", k=KD)
        O_T, R_T = r_b[:, 0:T], r_b[:, T:2 * T]
        r1 = sb("r1", [P, 8192])
        Qs = r1[:, 0:2048].rearrange("p (a n) -> p a n", a=NP0)
        KT = r1[:, 2048:4096].rearrange("p (a n) -> p a n", a=NP0)
        gate = r1[:, 4096:6144].rearrange("p (t n) -> p t n", t=TT)
        Kn = r1[:, 6144:8192].rearrange("p (c a n) -> p c a n", c=TT, a=NP0)
        probs = r1[:, :].rearrange("p (s n) -> p s n", s=8)
        hidden = r1[:, :].rearrange("p (h f n) -> p h f n", h=2, f=NF)
        r2 = sb("r2", [P, 4096])
        Qbd = r2[:, :].rearrange("p (a e n) -> p a e n", a=NP0, e=2)
        attn = r2[:, :].rearrange("p (g n) -> p g n", g=KV)
        r3 = sb("r3", [P, TT * NP0 * 3 * WIN])
        Vz = r3[:, :].rearrange("p (t a n) -> p t a n", t=TT, a=NP0)
        q_parts = r3[:, 0:3072].bitcast(BF16).rearrange("p (i m n) -> p i m n", i=3, m=KD)
        r4 = sb("r4", [P, 4096])
        t_exp = r4[:, 0:1024].rearrange("p (s n) -> p s n", s=2)
        t_rel = r4[:, 1024:2048].rearrange("p (s n) -> p s n", s=2)
        Am = r4[:, 2048:3072].rearrange("p (s n) -> p s n", s=4)
        y = r4[:, 3072:4096].rearrange("p (s n) -> p s n", s=2)
        mixed = r4[:, 0:2048].rearrange("p (j k n) -> p j k n", j=2, k=KD)
        k_rel = r4[:, 2048:3072].rearrange("p (s n) -> p s n", s=2)
        k_act = r4[:, 3072:4096].rearrange("p (k n) -> p k n", k=KD)
        k_parts = r4[0:64, 0:1536].bitcast(BF16).rearrange("p (i n) -> p i n", i=3)
        f_w = r4[:, 0:1024].rearrange("p (s n) -> p s n", s=2)
        f_n = r4[:, 1024:2048].rearrange("p (s n) -> p s n", s=2)
        f_s = r4[:, 2048:3072].rearrange("p (s n) -> p s n", s=2)
        f_z = r4[:, 3072:4096].rearrange("p (s n) -> p s n", s=2)
        r5 = sb("r5", [P, 1024])
        yT = r5[:, :].rearrange("p (s n) -> p s n", s=2)
        m_tmp = r5[:, :].rearrange("p (s n) -> p s n", s=2)
        sig = r5[:, 0:512].rearrange("p (s n) -> p s n", s=2)
        prod = r5[:, 512:1024].rearrange("p (s n) -> p s n", s=2)
        rest = r5[:, :].rearrange("p (s n) -> p s n", s=2)
        state = sb("state", [P, 2, NP0, 2 * WIN])
        q_stack = sb("q_stack", [KSTACK, 2, GR, T], BF16)
        k_stack = sb("k_stack", [KSTACK, KV, T], BF16)
        v_aug = sb("v_aug", [P, NT, KV, 2 * HD])
        neg2 = sb("neg2", [P, GR * NT, 2])
        neg = sb("neg", [P, GR * NT])
        m_parts = sb("m_parts", [32, 3, P], BF16)
        m_rest = sb("m_rest", [32, 2, P])
        sums = sb("sums", [32, 2, P])
        den = sb("den", [P, 2, 2, 4])
        ln_x = sb("ln_x", [P, 2, D])
        ln_s = sb("ln_s", [P, 2, 16])

        ps = [ctx.enter_context(nc.psum_tensor(f"bank{b}", [P, HALF], F32)) for b in range(4, 8)]
        ps03 = ctx.enter_context(nc.psum_tensor("banks", [P, 4, HALF], F32))
        bank = [ps03[:, i, :] for i in range(4)] + [t[:, :] for t in ps]
        order_of = {}
        for key in order:
            order_of.setdefault(key[0], []).append(key)

        def nth(key):
            return order_of[key[0]].index(key)

        def given_back(key):
            k = key[0]
            if k in ("xt", "x1", "x2", "x3"):
                return k, 2 * key[1] + key[2] + 1
            if k in ("g", "v", "yt", "w", "rv", "kn", "wo", "w2"):
                n = nth(key)
                return {"g": ("gz", n + 1), "v": ("vz", n + 1), "yt": ("yt", TT * key[1] + key[-1] + 1),
                        "w": ("ln_step", 2 * (TT * key[1] + key[-1]) + 1), "rv": ("rv_mul", n + 1), "kn": ("kn", n + 1),
                        "wo": ("ln_step", 2 * (16 + n) + 1), "w2": ("ln_step", 2 * (24 + n) + 1)}[k]
            if k in ("q", "k"):
                return "phi", 2 * (key[1] * NP0 + key[2]) + (k == "k") + 1
            if k in ("a", "u"):
                return {"a": "am", "u": "state"}[k], (key[1] * TT + key[2]) * NP0 + key[3] + 1
            if k == "o":
                return "o_div", nth(key) + 1
            if k == "kf":
                return "kr", 2 * key[1] + key[2] + 1
            if k in ("pq", "pk"):
                return "rest1", 3 * key[1] + (key[2] if k == "pq" else 2) + 1
            if k == "pv":
                return "v1", key[1] + 1
            if k == "mx":
                return "mx", 2 * (key[1] * GR * NT + key[2]) + key[3] + 1
            if k == "mt":
                return "mt_r", key[1] + 1
            if k == "s":
                return "p", (key[1] * NT + key[2]) * GR + key[3] + 1
            if k == "ot":
                return "o_copy", key[1] + 1
            assert k == "h"
            return "fz", key[1] * NF + key[2] + 1

        def take(pe, b, key):
            for last, turn in plan[key][1]:
                s, n = given_back(last)
                if turn:
                    pe.wait_ge(S[s], at(b, s, n))
                elif s in START:
                    pe.wait_ge(S[s], at(b, s, n - per[s]))

        def full(eng, b, key):
            banks, _, n = plan[key]
            eng.wait_ge(filled[banks[0]], b * uses[banks[0]] + n + 1)
            return [bank[k] for k in banks]

        def fills(key):
            return filled[plan[key][0][0]]

        def two_heads(window):
            return window.rearrange("p (w n) -> p w n", w=3)[:, 0:3:2, :]

        q_dram = nc.dram_tensor("q_scratch", [3, D, T], BF16).ap()
        k_dram = nc.dram_tensor("k_scratch", [3, KV * HD, T], BF16).ap()
        r_dram = nc.dram_tensor("r_scratch", [GR, T], F32).ap()
        x_v = A["x"].rearrange("b (t p) d -> b p t d", p=P)
        out_v = out.rearrange("b (t p) d -> b p t d", p=P)

        def ln_index(key):
            if key[0] == "wo":
                return 16 + key[1]
            return {"w": 0, "rv": 8, "w2": 24}[key[0]] + TT * key[1] + key[2]

        block = ctx.enter_context(nc.Block())

        N_LOADS = 30
        N_C_ACT, N_C_DVE = 18, 25

        back, ahead1, left = r4[:, 0:P], r4[:, P:2 * P], r4[:, 2 * P:2 * P + 1]

        def tmp(n):
            return r4[:, 272 + 8 * n:280 + 8 * n]

        @block.sync
        def _(sp):
            def load(dst, src):
                sp.dma_start(dst, src, allow_slow_non_contiguous=True).then_inc(loads, 16)

            for j, n in enumerate(("wq", "wk", "wv", "wg")):
                load(w_in[:, j], A[n].rearrange("(k p) n -> p k n", p=P))
            load(w_out[:], A["wo"].rearrange("(k p) n -> p k n", p=P))
            for j, n in enumerate(("fr", "fk", "fv")):
                load(w_ffn[:, j], A[n].rearrange("(k p) n -> p k n", p=P))
            load(w_q1[:], A["Wq"].rearrange("(k p) n -> p k n", p=P))
            load(w_vk1[:, :, 0:64], A["Wv"].rearrange("(k p) n -> p k n", p=P))
            load(w_vk1[:, :, 64:128], A["Wk"].rearrange("(k p) n -> p k n", p=P))
            load(w_o1[:], A["Wo"].rearrange("(k p) n -> p k n", p=P))
            load(w_f1[:], A["W1"].rearrange("(k p) n -> p k n", p=P))
            load(w_f2[:], A["W2"].rearrange("(k p) n -> p k n", p=P))
            load(gate_bias[:], A["gb"].partition_broadcast(P))
            load(bo_row[:], A["bo"].partition_broadcast(P))
            load(b2_row[:], A["b2"].partition_broadcast(P))
            load(bv_row[:], A["bv"].partition_broadcast(P))
            load(cols[:, 0:2], A["bq"].rearrange("(k p) -> p k", p=P))
            load(cols[0:64, 2:3], A["bk"].rearrange("(k p) -> p k", p=64))
            load(cols[:, 4:6], A["mu_r"].rearrange("(k p) -> p k", p=P))
            load(cols[:, 6:8], A["mu_k"].rearrange("(k p) -> p k", p=P))
            load(f_b1, A["b1"].rearrange("(k p) -> p k", p=P))
            load(f_turn, A["ph"].rearrange("(k p) -> p k", p=P))
            load(f_coef, A["wr"].rearrange("(k p) -> p k", p=P))
            load(tmp(0), A["wi"].rearrange("(k p) -> p k", p=P))
            load(lg, A["dl"].partition_broadcast(P))
            sp.wait_ge(c_pool, 3)
            for i in range(3):
                load(k_stack[96 + i:97 + i, :, :].rearrange("i k n -> i (k n)").rearrange("i (p n) -> i p n", p=32), m_parts[:, i, :])

            def fill_queries(b, g):
                for r, i in enumerate((0, 1, 2, 0, 1, 0)):
                    sp.dma_start(q_stack[16 * r:16 * r + 16, g % 2],
                                 q_dram[i, 64 * g:64 * g + 64, :].rearrange("(h d) n -> d h n", d=HD)).then_inc(S["qs%d" % (g % 2)], 16)

            with sp.Fori(0, NB) as b:
                sp.wait_ge(S["ln_step"], at(b, "ln_step", 2 * NT - 1 - per["ln_step"]))
                sp.dma_start(x_in[:], x_v[b]).then_inc(S["x_in"], 16)
                for key in order:
                    if key[0] == "stack":
                        sp.wait_ge(S["parts"], at(b, "parts", 6))
                        sp.dma_start(k_dram.rearrange("i p n -> p i n"), k_parts[:, :, :]).then_inc(S["k_out"], 16)
                        sp.dma_start(q_dram.rearrange("i (m p) n -> p i m n", p=P), q_parts[:, :, :, :]).then_inc(S["q_out"], 16)
                        sp.wait_ge(S["k_out"], at(b, "k_out", 16))
                        for r, i in enumerate((0, 0, 0, 1, 1, 2)):
                            sp.dma_start(k_stack[16 * r:16 * r + 16, :, :],
                                         k_dram[i].rearrange("(k d) n -> d k n", d=HD)).then_inc(S["ks"], 16)
                        sp.wait_ge(S["q_out"], at(b, "q_out", 16))
                        fill_queries(b, 0)
                        fill_queries(b, 1)
                    elif key[0] == "mt":
                        g = key[1]
                        sp.wait_ge(S["m_parts"], at(b, "m_parts", g + 1))
                        for i in range(3):
                            sp.dma_start(q_stack[96 + i:97 + i, g % 2].rearrange("i h n -> i (h n)").rearrange("i (p n) -> i p n", p=32),
                                         m_parts[:, i, :]).then_inc(S["m%d" % (g % 2)], 16)
                    elif key[0] == "ot":
                        g = key[1]
                        sp.wait_ge(S["o_copy"], at(b, "o_copy", g + 1))
                        if g + 2 < KV:
                            fill_queries(b, g + 2)
                        sp.dma_start(sums[:, 0, :], O_T[HD:P:32, :].rearrange("h (s n) -> h s n", n=P)).then_inc(S["sums"], 16)
                        sp.wait_ge(S["recip"], at(b, "recip", g + 1))
                        sp.dma_start(r_dram.rearrange("h (s n) -> (h s) n", n=P), sums[:, 1, :]).then_inc(S["r_out"], 16)
                        sp.wait_ge(S["r_out"], at(b, "r_out", 16 * (g + 1)))
                        if g:
                            sp.wait_ge(S["on"], at(b, "on", g))
                        for h in range(GR):
                            sp.dma_start(R_T[32 * h:32 * h + 32, :], r_dram[h, :].partition_broadcast(32)).then_inc(S["r_in"], 16)

        @block.gpsimd
        def _(pool):
            g = nc.gpsimd
            g.memset(ident[:], 0.0).then_inc(c_pool, 1)
            g.memset(m_parts[:], 1.0).then_inc(c_pool, 1)
            pool.wait_ge(c_pool, 2)
            g.affine_select(out=ident[:], in_=ident[:], compare_op=ALU.not_equal, fill=1.0, base=0,
                            pattern=[[-1, P]], channel_multiplier=1).then_inc(c_pool, 1)
            g.iota(back, pattern=[[1, P]], base=0, channel_multiplier=-1, allow_small_or_imprecise_dtypes=True).then_inc(c_pool, 1)
            g.iota(ahead1, pattern=[[1, P]], base=1, channel_multiplier=0, allow_small_or_imprecise_dtypes=True).then_inc(c_pool, 1)
            g.iota(left, pattern=[[0, 1]], base=P - 1, channel_multiplier=-1, allow_small_or_imprecise_dtypes=True).then_inc(c_pool, 1)
            g.memset(minus_half, -0.5).then_inc(c_pool, 1)
            g.memset(ln_eps, LN_EPS).then_inc(c_pool, 1)
            g.memset(v_aug[:], 1.0).then_inc(c_pool, 1)
            g.memset(state[:], 0.0).then_inc(c_pool, 1)
            g.memset(r_a[:, :, 0:1], 0.0).then_inc(c_pool, 1)
            pool.wait_ge(c_act, 2 + H0)
            g.affine_select(out=decay[:], in_=decay[:], compare_op=ALU.is_ge, fill=0.0, base=0,
                            pattern=[[0, H0], [1, P]], channel_multiplier=-1).then_inc(c_pool, 1)
            pool.wait_ge(c_act, N_C_ACT)
            pool.wait_ge(c_dve, N_C_DVE)
            for name, n in START.items():
                g.sem_inc(S[name], n)

            with pool.Fori(0, NB) as b:
                for key in order:
                    k = key[0]
                    if k == "init":
                        g.memset(r2[:], 0.0).then_inc(S["init"], 1)
                        g.memset(r3[:, :].rearrange("p (t n) -> p t n", n=3 * WIN)[:, :, WIN:2 * WIN], 0.0)
                        g.memset(r3[:, :].rearrange("p (t n) -> p t n", n=3 * WIN)[:, :, DK:DK + 1], 1.0)
                        g.memset(r3[:, :].rearrange("p (t n) -> p t n", n=3 * WIN)[:, :, 3 * WIN - 1:3 * WIN],
                                 1.0).then_inc(S["init"], 1)
                    elif k == "o":
                        _, h, c, pp = key
                        pool.wait_ge(S["o_div"], at(b, "o_div", nth(key) + 1))
                        pool.wait_ge(S["gate"], at(b, "gate", h * TT + c + 1))
                        ys = y[:, c % 2, 256 * pp:256 * pp + 256]
                        g.tensor_tensor(ys, ys, gate[:, c, 256 * pp:256 * pp + 256], ALU.mult).then_inc(S["y"], 1)
                    elif k in ("w", "rv", "wo", "w2"):
                        n = ln_index(key)
                        pool.wait_ge(S["ln_stat"], at(b, "ln_stat", n + 1))
                        v = ln_s[:, n % 2, 9:10]
                        g.tensor_tensor(v, ln_s[:, n % 2, 7:8], ln_eps, ALU.add).then_inc(S["ln_eps"], 1)
                        pool.wait_ge(S["ln_eps"], at(b, "ln_eps", n + 1))
                        g.tensor_tensor(ln_s[:, n % 2, 8:9], v, minus_half, ALU.pow).then_inc(S["ln_rstd"], 1)
                    elif k == "bo":
                        h = key[1]
                        pool.wait_ge(S["x2"], at(b, "x2", 2 * h + 2))
                        g.tensor_tensor(xn[:, h * TT:(h + 1) * TT, :], xn[:, h * TT:(h + 1) * TT, :],
                                        bo_row[:, :].unsqueeze(1).to_broadcast([P, TT, D]), ALU.add).then_inc(S["bo"], 1)
                    elif k == "b2":
                        pool.wait_ge(S["x3"], at(b, "x3", 4))
                        for h in range(2):
                            g.tensor_tensor(xn[:, h * TT:(h + 1) * TT, :], xn[:, h * TT:(h + 1) * TT, :],
                                            b2_row[:, :].unsqueeze(1).to_broadcast([P, TT, D]), ALU.add).then_inc(S["b2"], 1)
                    elif k == "on":
                        gr = key[1]
                        pool.wait_ge(S["r_in"], at(b, "r_in", 16 * GR * (gr + 1)))
                        g.tensor_tensor(attn[:, gr, :], O_T, R_T, ALU.mult).then_inc(S["on"], 1)
                    elif k == "h":
                        i = nth(key)
                        pool.wait_ge(S["fn"], at(b, "fn", i + 1))
                        g.tensor_tensor(f_n[:, i % 2, :], f_w[:, i % 2, :], f_n[:, i % 2, :], ALU.subtract).then_inc(S["fr"], 1)

        @block.scalar
        def _(act):
            a = nc.scalar.activation
            act.wait_ge(loads, 16 * N_LOADS)
            act.wait_ge(c_dve, 2)
            a(tmp(3), tmp(2), ACT.Exp, scale=-1.0).then_inc(c_act, 1)
            act.wait_ge(c_act, 1)
            a(tmp(4), tmp(3), ACT.Ln, bias=1.0).then_inc(c_act, 1)
            act.wait_ge(c_dve, 8)
            act.wait_ge(c_pool, 6)
            for h in range(H0):
                a(decay[:, h, :], back, ACT.Exp, scale=lg[:, h:h + 1]).then_inc(c_act, 1)
            for p in range(NP0):
                a(q_pow[:, p, :], ahead1, ACT.Exp, scale=lg_pair[:, p:p + 1]).then_inc(c_act, 1)
            a(c_pow[:], lg_pair, ACT.Exp, scale=float(P)).then_inc(c_act, 1)
            a(k_pow[:], lg, ACT.Exp, scale=left).then_inc(c_act, 1)
            act.wait_ge(c_dve, 20)
            a(tmp(5), tmp(9), ACT.Sin, scale=TURN).then_inc(c_act, 1)
            a(tmp(6), tmp(10), ACT.Sin, scale=TURN).then_inc(c_act, 1)

            with act.Fori(0, NB) as b:
                for key in order:
                    k = key[0]
                    if k in ("xt", "x1", "x2", "x3"):
                        _, h, kd = key
                        dst = {"xt": x0T[:, kd, :], "x1": x1T[:, kd, 1 + h * HALF:1 + (h + 1) * HALF],
                               "x2": x2T[:, kd, h * HALF:(h + 1) * HALF],
                               "x3": x3T[:, kd, 1 + h * HALF:1 + (h + 1) * HALF]}[k]
                        (src,) = full(act, b, key)
                        a(dst, src, ACT.Copy).then_inc(S[k], 1)
                    elif k == "g":
                        _, h, t = key
                        act.wait_ge(S["gz"], at(b, "gz", nth(key) + 1))
                        a(gate[:, t, :], gate[:, t, :], ACT.Sigmoid).then_inc(S["gate"], 1)
                    elif k == "v":
                        _, h, t = key
                        (src,) = full(act, b, key)
                        if t == 0 and h == 0:
                            act.wait_ge(S["init"], at(b, "init", 2))
                        a(Vz[:, t].rearrange("p a n -> p (a n)").rearrange("p (e n) -> p e n", n=WIN * 3)[:, :, 0:DK],
                          src.rearrange("p (a e n) -> p a e n", a=NP0, e=2)[:, :, 0, :], ACT.Copy)
                        a(Vz[:, t].rearrange("p a n -> p (a n)").rearrange("p (e n) -> p e n", n=WIN * 3)[:, :, 2 * WIN:2 * WIN + DK],
                          src.rearrange("p (a e n) -> p a e n", a=NP0, e=2)[:, :, 1, :], ACT.Copy).then_inc(S["vz"], 1)
                    elif k in ("q", "k"):
                        _, h, p = key
                        i = 2 * (h * NP0 + p) + (k == "k")
                        (src,) = full(act, b, key)
                        if i >= 2:
                            act.wait_ge(S["phi"], at(b, "phi", i - 1))
                        a(t_rel[:, i % 2, :], src, ACT.Relu, scale=-1.0).then_inc(S["neg"], 1)
                        act.wait_ge(S["neg"], at(b, "neg", i + 1))
                        a(t_exp[:, i % 2, :], t_rel[:, i % 2, :], ACT.Exp, scale=-1.0).then_inc(S["er"], 1)
                    elif k == "yt":
                        _, h, c = key
                        (src,) = full(act, b, key)
                        a(yT[:, c % 2, :], src, ACT.Copy).then_inc(S["yt"], 1)
                    elif k == "mix":
                        h = key[1]
                        act.wait_ge(S["x1"], at(b, "x1", 2 * h + 2))
                        if h:
                            act.wait_ge(S["ln_step"], at(b, "ln_step", 2 * (8 + TT - 1) + 1))
                        for j in range(4):
                            if j >= 2 or h:
                                act.wait_ge(S["mix"], at(b, "mix", 4 * h + j - 1))
                            a(m_tmp[:, j % 2, :], x1T[:, j % 2, h * HALF:(h + 1) * HALF], ACT.Copy,
                              scale=om[:, j:j + 1]).then_inc(S["mix_tmp"], 1)
                    elif k == "kf":
                        _, h, m = key
                        i = 2 * h + m
                        (src,) = full(act, b, key)
                        a(k_rel[:, m, :], src, ACT.Relu).then_inc(S["kr"], 1)
                        act.wait_ge(S["kr"], at(b, "kr", i + 1))
                        a(k_act[:, m, :], k_rel[:, m, :], ACT.Square).then_inc(S["ka"], 1)
                    elif k == "rv":
                        _, h, t = key
                        (src,) = full(act, b, key)
                        n = h * TT + t
                        if n >= 2:
                            act.wait_ge(S["rv_mul"], at(b, "rv_mul", n - 1))
                        a(sig[:, t % 2, :], src[:, 0:D], ACT.Sigmoid).then_inc(S["sg"], 1)
                    elif k == "pq":
                        _, h, m = key
                        (src,) = full(act, b, key)
                        a(q_parts[:, 0, m, h * HALF:(h + 1) * HALF], src, ACT.Identity, bias=bq[:, m:m + 1]).then_inc(S["part1"], 1)
                    elif k == "pk":
                        h = key[1]
                        (src,) = full(act, b, key)
                        a(k_parts[:, 0, h * HALF:(h + 1) * HALF], src[0:64, :], ACT.Identity, bias=bk).then_inc(S["part1"], 1)
                    elif k == "mt":
                        g = key[1]
                        (src,) = full(act, b, key)
                        if g:
                            act.wait_ge(S["m%d" % ((g - 1) % 2)], at(b, "m0", 48 * (1 + (g - 1) // 2)))
                        a(m_parts[:, 0, :], src[0:32, 0:P], ACT.Copy).then_inc(S["mt1"], 1)
                    elif k == "s":
                        _, g, c, h = key
                        full(act, b, key)
                        lo = 0 if h % 2 == 0 else 2
                        a(probs[:, 4 * (c % 2) + h, :], ps03[:, lo:lo + 2, :].rearrange("p a n -> p (a n)"), ACT.Exp,
                          scale=1.0 / HD ** 0.5).then_inc(S["p"], 1)
                    elif k == "ot":
                        g = key[1]
                        src = full(act, b, key)
                        if g:
                            act.wait_ge(S["on"], at(b, "on", g))
                        a(O_T[:, 0:HALF], src[0], ACT.Copy)
                        a(O_T[:, HALF:T], src[1], ACT.Copy).then_inc(S["o_copy"], 1)
                    elif k in ("h", "hb"):
                        if k == "h":
                            _, h, f = key
                            i = nth(key)
                            (src,) = full(act, b, key)
                            if i >= 2:
                                act.wait_ge(S["fr"], at(b, "fr", i - 1))
                            a(f_w[:, i % 2, :], src, ACT.Identity, bias=f_turn[:, f:f + 1], scale=0.1 / TWO_PI).then_inc(S["fw"], 1)
                        if k == "hb" or key[2]:
                            i = key[1] * NF + key[2] - (k == "h")
                            act.wait_ge(S["fr"], at(b, "fr", i + 1))
                            if i >= 2:
                                act.wait_ge(S["fz"], at(b, "fz", i - 1))
                            a(f_s[:, i % 2, :], f_n[:, i % 2, :], ACT.Sin, scale=TURN).then_inc(S["sin"], 1)
                    elif k == "out":
                        h = key[1]
                        act.wait_ge(S["ln_done"], at(b, "ln_done", 24 + TT * (h + 1)))
                        act.dma_start(out_v[b][:, h * TT:(h + 1) * TT, :], xn[:, h * TT:(h + 1) * TT, :]).then_inc(S["out"], 16)
            act.wait_ge(S["out"], at(NB, "out", 0))

        @block.vector
        def _(dve):
            v = nc.vector
            steps = [0]

            def then(ins):
                steps[0] += 1
                ins.then_inc(c_dve, 1)
                dve.wait_ge(c_dve, steps[0])

            dve.wait_ge(loads, 16 * N_LOADS)
            then(v.tensor_scalar(tmp(1), lg, -1.0, None, ALU.mult))
            then(v.tensor_tensor(tmp(2), tmp(1), lg, ALU.max))
            then(v.tensor_scalar(tmp(1), lg, 0.0, None, ALU.min))
            dve.wait_ge(c_act, 2)
            then(v.tensor_tensor(lg, tmp(1), tmp(4), ALU.subtract))
            then(v.tensor_copy(lg_pair[0:64], lg[0:64, 0:H0:2]))
            then(v.tensor_copy(lg_pair[64:128], lg[64:128, 1:H0:2]))
            dve.wait_ge(c_pool, 4)
            then(v.tensor_scalar(back, back, 0.0, None, ALU.max))
            then(v.tensor_scalar(om, mu, -1.0, 1.0, ALU.mult, ALU.add))
            then(v.tensor_scalar(tmp(7), f_turn, 1.0 / TWO_PI, MAGIC, ALU.mult, ALU.add))
            then(v.tensor_scalar(tmp(7), tmp(7), MAGIC, None, ALU.subtract))
            for part in (PI_A, PI_B, PI_C):
                then(v.scalar_tensor_tensor(f_turn, tmp(7), -part, f_turn, ALU.mult, ALU.add))
            then(v.tensor_scalar(f_turn, f_turn, 1.0 / TWO_PI, None, ALU.mult))
            then(v.tensor_scalar(tmp(8), f_turn, MAGIC, MAGIC, ALU.add, ALU.subtract))
            then(v.tensor_tensor(tmp(9), f_turn, tmp(8), ALU.subtract))
            then(v.tensor_scalar(tmp(10), f_turn, 0.25, None, ALU.add))
            then(v.tensor_scalar(tmp(8), tmp(10), MAGIC, MAGIC, ALU.add, ALU.subtract))
            then(v.tensor_tensor(tmp(10), tmp(10), tmp(8), ALU.subtract))
            then(v.scalar_tensor_tensor(f_turn, f_b1, 0.1 / TWO_PI, f_turn, ALU.mult, ALU.add))
            dve.wait_ge(c_act, N_C_ACT)
            then(v.tensor_tensor(tmp(6), tmp(6), f_coef, ALU.mult))
            then(v.tensor_tensor(tmp(5), tmp(5), tmp(0), ALU.mult))
            then(v.tensor_tensor(tmp(5), tmp(5), tmp(6), ALU.add))
            then(v.tensor_tensor(tmp(5), tmp(5), tmp(0), ALU.mult))
            then(v.tensor_scalar(f_coef, tmp(5), 0.1, None, ALU.mult))
            dve.wait_ge(c_pool, 12)

            def norm_stats(b, n, psum, resid, key):
                xs, st = ln_x[:, n % 2, :], ln_s[:, n % 2, :]
                if n >= 2:
                    dve.wait_ge(S["ln_done"], at(b, "ln_done", n - 1))
                v.tensor_tensor(xs, resid, psum, ALU.add).then_inc(S["ln_step"], 1)
                dve.wait_ge(S["ln_step"], at(b, "ln_step", 2 * n + 1))
                v.bn_stats(st[:, 0:6], xs).then_inc(S["ln_step"], 1)
                dve.wait_ge(S["ln_step"], at(b, "ln_step", 2 * n + 2))
                v.memset(st[:, 10:11], 0.0)
                v.bn_aggr(st[:, 6:8], st[:, 0:6]).then_inc(S["ln_stat"], 1)

            with dve.Fori(0, NB) as b:
                for key in order:
                    k = key[0]
                    if k == "g":
                        _, h, t = key
                        (src,) = full(dve, b, key)
                        if h:
                            dve.wait_ge(S["y"], at(b, "y", 2 * (t + 1)))
                        v.tensor_tensor(gate[:, t, :], src, gate_bias[:], ALU.add).then_inc(S["gz"], 1)
                    elif k in ("q", "k"):
                        _, h, p = key
                        i = 2 * (h * NP0 + p) + (k == "k")
                        (src,) = full(dve, b, key)
                        dve.wait_ge(S["er"], at(b, "er", i + 1))
                        if k == "k":
                            v.scalar_tensor_tensor(KT[:, p, :], src, 0.0, t_exp[:, i % 2, :], ALU.max, ALU.add).then_inc(S["phi"], 1)
                        else:
                            if i == 0:
                                dve.wait_ge(S["init"], at(b, "init", 1))
                            v.scalar_tensor_tensor(Qbd[0:64, p, 0, :], src[0:64], 0.0, t_exp[0:64, i % 2, :],
                                                   ALU.max, ALU.add)
                            v.scalar_tensor_tensor(Qbd[64:128, p, 1, :], src[64:128], 0.0, t_exp[64:128, i % 2, :],
                                                   ALU.max, ALU.add).then_inc(S["phi"], 1)
                            dve.wait_ge(S["phi"], at(b, "phi", i + 1))
                            for e in range(2):
                                rows = slice(64 * e, 64 * e + 64)
                                last = v.tensor_tensor(Qs[rows, p, :].rearrange("p (c n) -> p c n", c=TT),
                                                       Qbd[rows, p, e, :].rearrange("p (c n) -> p c n", c=TT),
                                                       q_pow[rows, p, :].unsqueeze(1).to_broadcast([64, TT, P]), ALU.mult)
                            last.then_inc(S["qs"], 1)
                    elif k == "kn":
                        _, h, p = key
                        (src,) = full(dve, b, key)
                        v.tensor_tensor(Kn[:, :, p, :].rearrange("p c (e n) -> p c e n", e=2),
                                        src.rearrange("p (c e n) -> p c e n", c=TT, e=2),
                                        k_pow[:, 2 * p:2 * p + 2].unsqueeze(1).unsqueeze(3).to_broadcast([P, TT, 2, DK]),
                                        ALU.mult).then_inc(S["kn"], 1)
                    elif k == "a":
                        _, h, c, pp = key
                        for j in range(2):
                            p = 2 * pp + j
                            sub = ("a", h, c, p)
                            (src,) = full(dve, b, sub)
                            v.tensor_tensor(Am[:, p, :], src[:, 0:2 * P],
                                            decay[:, 2 * p:2 * p + 2, :].rearrange("p e n -> p (e n)"), ALU.mult).then_inc(S["am"], 1)
                    elif k == "u":
                        _, h, c, pp = key
                        for j in range(2):
                            p = 2 * pp + j
                            (src,) = full(dve, b, ("u", h, c, p))
                            now, new = c % 2, (c + 1) % 2
                            for e in range(2):
                                rows, cs = slice(64 * e, 64 * e + 64), slice(WIN * e, WIN * e + WIN)
                                if (h, c) == (0, 0):
                                    last = v.tensor_copy(state[rows, new, p, cs], src[rows, cs])
                                else:
                                    if e == 0:
                                        dve.wait_ge(S["state"], at(b, "state", (h * TT + c - 1) * NP0 + p + 1))
                                    last = v.scalar_tensor_tensor(state[rows, new, p, cs], state[rows, now, p, cs],
                                                                  c_pow[rows, p:p + 1], src[rows, cs], ALU.mult, ALU.add)
                            last.then_inc(S["state"], 1)
                    elif k == "o":
                        _, h, c, pp = key
                        n = nth(key)
                        (src,) = full(dve, b, key)
                        heads = src[:, 0:4 * WIN].rearrange("p (e n) -> p e n", n=WIN)
                        v.tensor_scalar(den[:, n % 2, 0, :], heads[:, :, DK], DEN_EPS, None, ALU.add).then_inc(S["o_step"], 1)
                        dve.wait_ge(S["o_step"], at(b, "o_step", 2 * n + 1))
                        v.reciprocal(den[:, n % 2, 1, :], den[:, n % 2, 0, :]).then_inc(S["o_step"], 1)
                        dve.wait_ge(S["o_step"], at(b, "o_step", 2 * n + 2))
                        v.tensor_tensor(y[:, c % 2, 256 * pp:256 * pp + 256].rearrange("p (e n) -> p e n", e=4), heads[:, :, 0:DK],
                                        den[:, n % 2, 1, :].unsqueeze(2).to_broadcast([P, 4, DK]), ALU.mult).then_inc(S["o_div"], 1)
                    elif k == "w":
                        _, h, c = key
                        t = h * TT + c
                        (src,) = full(dve, b, key)
                        if t == 0:
                            dve.wait_ge(S["x_in"], at(b, "x_in", 16))
                            dve.wait_ge(S["out"], at(b, "out", 0))
                        norm_stats(b, t, src[:, 0:D], x_in[:, t, :], key)
                    elif k == "mix":
                        h = key[1]
                        for j in range(4):
                            dve.wait_ge(S["mix_tmp"], at(b, "mix_tmp", 4 * h + j + 1))
                            v.scalar_tensor_tensor(mixed[:, j // 2, j % 2, :], x1T[:, j % 2, 1 + h * HALF:1 + (h + 1) * HALF],
                                                   mu[:, j:j + 1], m_tmp[:, j % 2, :], ALU.mult, ALU.add).then_inc(S["mix"], 1)
                    elif k == "rv":
                        _, h, t = key
                        n = h * TT + t
                        dve.wait_ge(S["sg"], at(b, "sg", n + 1))
                        (src,) = full(dve, b, key)
                        if n >= 2:
                            dve.wait_ge(S["ln_step"], at(b, "ln_step", 2 * (8 + n - 2) + 1))
                        v.tensor_tensor(prod[:, t % 2, :], sig[:, t % 2, :], src[:, D:2 * D], ALU.mult).then_inc(S["rv_mul"], 1)
                        dve.wait_ge(S["rv_mul"], at(b, "rv_mul", n + 1))
                        norm_stats(b, 8 + n, prod[:, t % 2, :], xn[:, n, :], key)
                    elif k in ("pq", "pk"):
                        i = 3 * key[1] + (key[2] if k == "pq" else 2)
                        (src,) = full(dve, b, key)
                        h = key[1]
                        cut = slice(h * HALF, (h + 1) * HALF)
                        if k == "pq":
                            src, bias, parts, left_over = src, bq[:, key[2]:key[2] + 1], [q_parts[:, j, key[2], cut] for j in range(3)], rest[:, i % 2, :]
                        else:
                            src, bias, parts, left_over = src[0:64], bk, [k_parts[:, j, cut] for j in range(3)], rest[0:64, i % 2, :]
                        dve.wait_ge(S["part1"], at(b, "part1", i + 1))
                        v.scalar_tensor_tensor(left_over, src, bias, parts[0], ALU.add, ALU.subtract).then_inc(S["rest1"], 1)
                        dve.wait_ge(S["rest1"], at(b, "rest1", i + 1))
                        v.tensor_copy(parts[1], left_over).then_inc(S["part2"], 1)
                        dve.wait_ge(S["part2"], at(b, "part2", i + 1))
                        v.tensor_tensor(parts[2], left_over, parts[1], ALU.subtract).then_inc(S["parts"], 1)
                    elif k == "pv":
                        h = key[1]
                        (src,) = full(dve, b, key)
                        v.tensor_tensor(v_aug[:, h * TT:(h + 1) * TT, :, 0:HD],
                                        src.rearrange("p (t n) -> p t n", t=TT)[:, :, 0:KV * HD].rearrange("p t (k d) -> p t k d", k=KV),
                                        bv_row[:, :].rearrange("p (k d) -> p k d", k=KV).unsqueeze(1).to_broadcast([P, TT, KV, HD]),
                                        ALU.add).then_inc(S["v1"], 1)
                    elif k == "mx":
                        _, g, n = key
                        for j in range(2):
                            (src,) = full(dve, b, key + (j,))
                            v.tensor_reduce(neg2[:, n, j:j + 1], src, AX.X, ALU.max, negate=True).then_inc(S["mx"], 1)
                        if n == GR * NT - 1:
                            dve.wait_ge(S["mx"], at(b, "mx", 2 * (g + 1) * GR * NT))
                            v.tensor_tensor(neg[:], neg2[:, :, 0], neg2[:, :, 1], ALU.min).then_inc(S["nm"], 1)
                    elif k == "mt":
                        g = key[1]
                        (src,) = full(dve, b, key)
                        m_rest1, m_rest2 = m_rest[:, 0, :], m_rest[:, 1, :]
                        dve.wait_ge(S["mt1"], at(b, "mt1", g + 1))
                        v.tensor_tensor(m_rest1, src[0:32, 0:P], m_parts[:, 0, :], ALU.subtract).then_inc(S["mt_r"], 1)
                        dve.wait_ge(S["mt_r"], at(b, "mt_r", g + 1))
                        v.tensor_copy(m_parts[:, 1, :], m_rest1).then_inc(S["mt2"], 1)
                        dve.wait_ge(S["mt2"], at(b, "mt2", g + 1))
                        v.tensor_tensor(m_parts[:, 2, :], m_rest1, m_parts[:, 1, :], ALU.subtract).then_inc(S["m_parts"], 1)
                    elif k == "on":
                        g = key[1]
                        dve.wait_ge(S["sums"], at(b, "sums", 16 * (g + 1)))
                        v.reciprocal(sums[:, 1, :], sums[:, 0, :]).then_inc(S["recip"], 1)
                    elif k == "wo":
                        t = key[1]
                        if t % TT == 0:
                            dve.wait_ge(S["bo"], at(b, "bo", t // TT + 1))
                        (src,) = full(dve, b, key)
                        norm_stats(b, 16 + t, src[:, 0:D], xn[:, t, :], key)
                    elif k in ("h", "hb"):
                        if k == "h":
                            i = nth(key)
                            dve.wait_ge(S["fw"], at(b, "fw", i + 1))
                            if i >= 2:
                                dve.wait_ge(S["sin"], at(b, "sin", i - 1))
                            v.tensor_scalar(f_n[:, i % 2, :], f_w[:, i % 2, :], MAGIC, MAGIC, ALU.add, ALU.subtract).then_inc(S["fn"], 1)
                        if k == "hb" or key[2]:
                            h, f = key[1], key[2] - (k == "h")
                            i = h * NF + f
                            dve.wait_ge(S["sin"], at(b, "sin", i + 1))
                            (src,) = full(dve, b, ("h", h, f))
                            v.scalar_tensor_tensor(f_z[:, i % 2, :], f_s[:, i % 2, :], f_coef[:, f:f + 1], src,
                                                   ALU.mult, ALU.add).then_inc(S["fz"], 1)
                            dve.wait_ge(S["fz"], at(b, "fz", i + 1))
                            v.tensor_scalar(hidden[:, h, f, :], f_z[:, i % 2, :], f_b1[:, f:f + 1], 0.0, ALU.add, ALU.max).then_inc(S["act"], 1)
                    elif k == "w2":
                        _, h, t = key
                        n = h * TT + t
                        if t == 0:
                            dve.wait_ge(S["b2"], at(b, "b2", h + 1))
                        (src,) = full(dve, b, key)
                        norm_stats(b, 24 + n, src[:, 0:D], xn[:, n, :], key)
                    elif k == "nb":
                        n = 8 * key[1] + key[2]
                        dve.wait_ge(S["ln_rstd"], at(b, "ln_rstd", n + 1))
                        v.tensor_scalar(xn[:, n % 8, :], ln_x[:, n % 2, :], ln_s[:, n % 2, 6:7], ln_s[:, n % 2, 8:9],
                                        ALU.subtract, ALU.mult).then_inc(S["ln_done"], 1)

        @block.tensor
        def _(pe):
            mm = nc.tensor.matmul

            def product(dst, terms):
                for i, (lhsT, rhs) in enumerate(terms):
                    last = mm(dst, lhsT, rhs, start=(i == 0), stop=(i == len(terms) - 1))
                return last

            def turn(key, tiles):
                (o,) = [bank[k] for k in plan[key][0]]
                for i, t in enumerate(tiles):
                    last = nc.tensor.transpose(o[0:t.shape[1], i * P:i * P + t.shape[0]], t, ident[:])
                last.then_inc(fills(key), 1)

            pe.wait_ge(c_pool, 12)
            pe.wait_ge(c_dve, N_C_DVE)
            with pe.Fori(0, NB) as b:
                for key in order:
                    k = key[0]
                    if k == "xt":
                        _, h, kd = key
                        pe.wait_ge(S["x_in"], at(b, "x_in", 16))
                        take(pe, b, key)
                        turn(key, [x_in[:, h * TT + t, kd * P:(kd + 1) * P] for t in range(TT)])
                    elif k in ("x1", "x2", "x3"):
                        _, h, kd = key
                        stage = int(k[1]) - 1
                        pe.wait_ge(S["ln_done"], at(b, "ln_done", 8 * stage + TT * (h + 1)))
                        take(pe, b, key)
                        turn(key, [xn[:, h * TT + t, kd * P:(kd + 1) * P] for t in range(TT)])
                    elif k in ("g", "v"):
                        _, h, t = key
                        pe.wait_ge(S["xt"], at(b, "xt", 2 * h + 2))
                        take(pe, b, key)
                        w = w_in[:, 3 if k == "g" else 2]
                        product(bank[plan[key][0][0]], [(x0T[:, kd, t * P:(t + 1) * P], w[:, kd, :]) for kd in range(KD)])\
                            .then_inc(fills(key), 1)
                    elif k in ("q", "k"):
                        _, h, p = key
                        take(pe, b, key)
                        w = w_in[:, 0 if k == "q" else 1]
                        product(bank[plan[key][0][0]], [(w[:, kd, p * P:(p + 1) * P], x0T[:, kd, :]) for kd in range(KD)])\
                            .then_inc(fills(key), 1)
                    elif k == "kn":
                        _, h, p = key
                        pe.wait_ge(S["phi"], at(b, "phi", 2 * (h * NP0 + p) + 2))
                        take(pe, b, key)
                        turn(key, [KT[:, p, c * P:(c + 1) * P] for c in range(TT)])
                    elif k == "a":
                        _, h, c, pp = key
                        for j in range(2):
                            p = 2 * pp + j
                            sub = ("a", h, c, p)
                            if c == 0:
                                pe.wait_ge(S["phi"], at(b, "phi", 2 * (h * NP0 + p) + 2))
                            take(pe, b, sub)
                            product(bank[plan[sub][0][0]][:, 0:2 * P].rearrange("p (e n) -> p e n", e=2),
                                    [(KT[:, p, c * P:(c + 1) * P], Qbd[:, p, :, c * P:(c + 1) * P])]).then_inc(fills(sub), 1)
                    elif k == "u":
                        _, h, c, pp = key
                        for j in range(2):
                            p = 2 * pp + j
                            sub = ("u", h, c, p)
                            if c == 0:
                                pe.wait_ge(S["kn"], at(b, "kn", h * NP0 + p + 1))
                                pe.wait_ge(S["vz"], at(b, "vz", (h + 1) * TT))
                            take(pe, b, sub)
                            product(bank[plan[sub][0][0]][:, 0:2 * WIN].rearrange("p (w n) -> p w n", w=2),
                                    [(Kn[:, c, p, :], two_heads(Vz[:, c, p, :]))]).then_inc(fills(sub), 1)
                    elif k == "o":
                        _, h, c, pp = key
                        take(pe, b, key)
                        o = bank[plan[key][0][0]]
                        if pp == 0:
                            pe.wait_ge(S["vz"], at(b, "vz", h * TT + c + 1))
                        for j in range(2):
                            p = 2 * pp + j
                            pe.wait_ge(S["am"], at(b, "am", (h * TT + c) * NP0 + p + 1))
                            terms = [(Am[:, p, e * P:(e + 1) * P], Vz[:, c, p, e * WIN:(e + 2) * WIN]) for e in range(2)]
                            if (h, c) != (0, 0):
                                if c == 0:
                                    pe.wait_ge(S["qs"], at(b, "qs", h * NP0 + p + 1))
                                pe.wait_ge(S["state"], at(b, "state", (h * TT + c - 1) * NP0 + p + 1))
                                terms.append((Qs[:, p, c * P:(c + 1) * P], state[:, c % 2, p, :]))
                            last = product(o[:, j * 2 * WIN:(j + 1) * 2 * WIN], terms)
                        last.then_inc(fills(key), 1)
                    elif k == "yt":
                        _, h, c = key
                        pe.wait_ge(S["y"], at(b, "y", 2 * (h * TT + c + 1)))
                        take(pe, b, key)
                        turn(key, [y[:, c % 2, f * P:(f + 1) * P] for f in range(4)])
                    elif k == "w":
                        _, h, c = key
                        pe.wait_ge(S["yt"], at(b, "yt", h * TT + c + 1))
                        take(pe, b, key)
                        product(bank[plan[key][0][0]][:, 0:D],
                                [(yT[:, c % 2, f * P:(f + 1) * P], w_out[:, f, :]) for f in range(4)]).then_inc(fills(key), 1)
                    elif k == "kf":
                        _, h, m = key
                        pe.wait_ge(S["mix"], at(b, "mix", 4 * h + 4))
                        take(pe, b, key)
                        product(bank[plan[key][0][0]],
                                [(w_ffn[:, 1, kd, m * P:(m + 1) * P], mixed[:, 1, kd, :]) for kd in range(KD)]).then_inc(fills(key), 1)
                    elif k == "rv":
                        _, h, t = key
                        take(pe, b, key)
                        o = bank[plan[key][0][0]]
                        ts = slice(t * P, (t + 1) * P)
                        product(o[:, 0:D], [(mixed[:, 0, kd, ts], w_ffn[:, 0, kd, :]) for kd in range(KD)])
                        if t == 0:
                            pe.wait_ge(S["ka"], at(b, "ka", 2 * h + 2))
                        product(o[:, D:2 * D], [(k_act[:, kd, ts], w_ffn[:, 2, kd, :]) for kd in range(KD)]).then_inc(fills(key), 1)
                    elif k == "pq":
                        _, h, m = key
                        pe.wait_ge(S["x2"], at(b, "x2", 2 * h + 2))
                        take(pe, b, key)
                        product(bank[plan[key][0][0]],
                                [(w_q1[:, kd, m * P:(m + 1) * P], x2T[:, kd, h * HALF:(h + 1) * HALF]) for kd in range(KD)])\
                            .then_inc(fills(key), 1)
                    elif k == "pk":
                        h = key[1]
                        take(pe, b, key)
                        product(bank[plan[key][0][0]][0:64, :],
                                [(w_vk1[:, kd, 64:128], x2T[:, kd, h * HALF:(h + 1) * HALF]) for kd in range(KD)]).then_inc(fills(key), 1)
                    elif k == "pv":
                        h = key[1]
                        take(pe, b, key)
                        for t in range(TT):
                            last = product(bank[plan[key][0][0]][:, t * P:(t + 1) * P],
                                           [(x2T[:, kd, (h * TT + t) * P:(h * TT + t + 1) * P], w_vk1[:, kd, :]) for kd in range(KD)])
                        last.then_inc(fills(key), 1)
                    elif k == "mx":
                        _, g, n = key
                        h, t = n // NT, n % NT
                        if n == 0:
                            pe.wait_ge(S["ks"], at(b, "ks", 96))
                            pe.wait_ge(S["qs%d" % (g % 2)], at(b, "qs0", 96 * (g // 2 + 1)))
                        for j in range(2):
                            take(pe, b, key + (j,))
                            mm(bank[plan[key + (j,)][0][0]], q_stack[0:96, g % 2, h, t * P:(t + 1) * P],
                               k_stack[0:96, g, j * HALF:(j + 1) * HALF], start=True, stop=True).then_inc(fills(key + (j,)), 1)
                    elif k == "mt":
                        g = key[1]
                        pe.wait_ge(S["nm"], at(b, "nm", g + 1))
                        take(pe, b, key)
                        turn(key, [neg[:]])
                    elif k == "s":
                        _, g, c, h = key
                        if c == 0 and h == 0:
                            pe.wait_ge(S["m%d" % (g % 2)], at(b, "m0", 48 * (g // 2 + 1)))
                        take(pe, b, key)
                        banks = plan[key][0]
                        for j in range(2):
                            last = mm(bank[banks[j]], k_stack[:, g, c * P:(c + 1) * P], q_stack[:, g % 2, h, j * HALF:(j + 1) * HALF],
                                      start=True, stop=True)
                        last.then_inc(fills(key), 1)
                    elif k == "av":
                        _, g, c = key
                        if c == 0:
                            take(pe, b, ("ot", g))
                            if g == 0:
                                pe.wait_ge(S["v1"], at(b, "v1", 2))
                        pe.wait_ge(S["p"], at(b, "p", (g * NT + c + 1) * GR))
                        for j in range(2):
                            for h in range(GR):
                                last = mm(bank[6 + j][32 * h:32 * h + 32, :], v_aug[:, c, g, :],
                                          probs[:, 4 * (c % 2) + h, j * HALF:(j + 1) * HALF], start=(c == 0), stop=(c == NT - 1))
                        if c == NT - 1:
                            last.then_inc(fills(("ot", g)), 1)
                    elif k == "wo":
                        t = key[1]
                        if t == 0:
                            pe.wait_ge(S["on"], at(b, "on", KV))
                        take(pe, b, key)
                        product(bank[plan[key][0][0]][:, 0:D],
                                [(attn[:, g, t * P:(t + 1) * P], w_o1[:, g, :]) for g in range(KV)]).then_inc(fills(key), 1)
                    elif k == "h":
                        _, h, f = key
                        if f == 0:
                            pe.wait_ge(S["x3"], at(b, "x3", 2 * h + 2))
                        take(pe, b, key)
                        product(bank[plan[key][0][0]],
                                [(w_f1[:, kd, f * P:(f + 1) * P], x3T[:, kd, 1 + h * HALF:1 + (h + 1) * HALF]) for kd in range(KD)])\
                            .then_inc(fills(key), 1)
                    elif k == "w2":
                        _, h, t = key
                        if t == 0:
                            pe.wait_ge(S["act"], at(b, "act", NF * (h + 1)))
                        take(pe, b, key)
                        product(bank[plan[key][0][0]][:, 0:D],
                                [(hidden[:, h, f, t * P:(t + 1) * P], w_f2[:, f, :]) for f in range(NF)]).then_inc(fills(key), 1)


INPUTS = {
    "x": "L0_attn_x", "wq": "L0_attn_W_Q", "wk": "L0_attn_W_K", "wv": "L0_attn_W_V", "wg": "L0_attn_W_g_w",
    "gb": "L0_attn_W_g_b", "wo": "L0_attn_W_O", "dl": "L0_attn_decay_log", "fr": "L0_ffn_W_r", "fk": "L0_ffn_W_k",
    "fv": "L0_ffn_W_v", "mu_r": "L0_ffn_mu_r", "mu_k": "L0_ffn_mu_k", "Wq": "L1_attn_Wq", "bq": "L1_attn_bq",
    "Wk": "L1_attn_Wk", "bk": "L1_attn_bk", "Wv": "L1_attn_Wv", "bv": "L1_attn_bv", "Wo": "L1_attn_Wo",
    "bo": "L1_attn_bo", "W1": "L1_ffn_W1", "b1": "L1_ffn_b1", "ph": "L1_ffn_quantum_phases",
    "wr": "L1_ffn_quantum_weights_real", "wi": "L1_ffn_quantum_weights_imag", "W2": "L1_ffn_W2", "b2": "L1_ffn_b2",
}
TRANSPOSED = ("wq", "wk", "wv", "wg", "wo", "fr", "fk", "fv")


def kernel(**inputs):
    import concourse.bacc as bacc
    from concourse.bass_utils import run_bass_kernel_spmd

    nc = bacc.Bacc("TRN2", target_bir_lowering=False, num_devices=1,
                    dynamic_dma_scratch_size=1024)
    arrays, A = {}, {}
    for name, long in INPUTS.items():
        a = np.asarray(inputs[long])
        if name in TRANSPOSED:
            a = a.T
        if name == "Wo":
            padded = np.zeros((KV, GR, 2 * HD, D), a.dtype)
            padded[:, :, :HD] = a.reshape(GR, KV, HD, D).transpose(1, 0, 2, 3)
            a = padded.reshape(KV * P, D)
        a = np.ascontiguousarray(a)
        arrays[name] = a
        A[name] = nc.dram_tensor(name, a.shape, mybir.dt.from_np(a.dtype), kind="ExternalInput").ap()
    shape = arrays["x"].shape
    out = nc.dram_tensor("out", shape, F32, kind="ExternalOutput").ap()
    nc.disable_value_cache = True
    program(nc, A, out)
    r = run_bass_kernel_spmd(nc, [arrays], core_ids=[0])
    return r.results[0]["out"]
```

```python
from contextlib import ExitStack
from typing import NamedTuple

import numpy as np

import concourse.bass as bass
from concourse import mybir

F32 = mybir.dt.float32
BF16 = mybir.dt.bfloat16
ACT = mybir.ActivationFunctionType
ALU = mybir.AluOpType
AX = mybir.AxisListType

P = 128
T = 1024
D = 256
KD = D // P
HALF = 512
TT = HALF // P
NT = T // P
H0, DK = 8, 64
NP0 = H0 * DK // P
WIN = DK + 1
KV, GR, HD = 4, 4, 16
NF = 1024 // P
MX_START = 10
MX_END = 8
MX_AHEAD = 12
KSTACK = 99
LN_EPS = 1e-5
DEN_EPS = 1e-6
MAGIC = 12582912.0
TWO_PI = 6.283185307179586
TURN = 6.2831850
PI_A, PI_B = 6.28125, 0.0019350051879882812
PI_C = TWO_PI - PI_A - PI_B


def sequence_order():
    o = []

    def project(h):
        if h == 0:
            o.extend(("xt", h, k) for k in range(KD))
            o.extend([("nb_last", 6), ("nb_last", 7)])
        for p in range(NP0):
            o.extend([("q", h, p), ("k", h, p)])
            if h == 1 and p == 0:
                o.append(("yt", 0, 3))
            if h == 1 and p == 1:
                o.extend([("w", 0, 3), ("nb", 0, 2)])
            if h == 1 and p == 2:
                o.append(("nb", 0, 3))
            if p:
                o.append(("kn", h, p - 1))
            o.extend([("g", h, p), ("v", h, p)])
        o.extend([("kn", h, NP0 - 1), ("sg", h)])

    def recur(h):
        steps = [(c, pp) for c in range(TT) for pp in range(2)]
        o.append(("a", h, *steps[0]))
        for n, (c, pp) in enumerate(steps):
            if n + 1 < len(steps):
                o.append(("a", h, *steps[n + 1]))
            if (h, c) != (1, TT - 1):
                o.append(("u", h, c, pp))
            if pp == 1 and c >= 1:
                o.append(("yt", h, c - 1))
            o.append(("o", h, c, pp))
            if pp == 1 and c >= 1:
                o.append(("w", h, c - 1))
                if c >= 2:
                    o.append(("nb", 0, h * TT + c - 2))
            if (h, c, pp) == (0, TT - 1, 0):
                o.extend(("xt", 1, k) for k in range(KD))
            if (h, c, pp) == (1, 1, 1):
                o.extend(("x1", 0, k) for k in range(KD))
            if h == 1 and 3 <= 2 * c + pp <= 6:
                o.append(("mix", 0, 2 * c + pp - 3))

    o.append(("init",))
    project(0)
    recur(0)
    project(1)
    recur(1)
    o.extend([("yt", 1, 3), ("kf", 0, 0), ("w", 1, 3), ("nb", 0, 6), ("kf", 0, 1), ("nb", 0, 7)])
    for h in range(2):
        if h == 1:
            o.extend([("kf", 1, 0), ("kf", 1, 1), ("nb", 1, 3)])
        for t in range(TT):
            if (h, t) == (1, TT - 1):
                o.extend(("x2", 0, k) for k in range(KD))
            o.append(("rv", h, t))
            if t:
                o.append(("nb", 1, h * TT + t - 1))
            if (h, t) == (0, 0):
                o.extend(("x1", 1, k) for k in range(KD))
                o.extend(("mix", 1, j) for j in range(4))
    o.append(("nb", 1, 7))
    for h in range(2):
        o.extend(("pq", h, m) for m in range(KD))
        o.append(("pk", h))
        if h == 0:
            o.extend(("x2", 1, k) for k in range(KD))
        o.extend([("pv", h), ("bo", h)])
    o.append(("stack",))

    def merge(main, maxima):
        weights = [WEIGHT.get(key[0], 0.0) for key in main]
        total, done, taken, n = sum(weights), 0.0, 0, len(maxima)
        for key, weight in zip(main, weights):
            o.append(key)
            done += weight
            while maxima and taken < done / total * n - 0.01:
                o.append(maxima.pop(0))
                taken += 1
        o.extend(maxima)

    def maxima(g):
        return [("mx", g, n, j) for n in range(GR * NT) for j in range(2)]

    ff = feed_forward_order()
    pieces = [i for i, key in enumerate(ff) if key[0] in ("h0", "h", "w20", "w2p", "w2")]
    start, end = pieces[MX_START], pieces[-MX_END]
    o.extend(ff[:start])
    merge(ff[start:end], maxima(0))
    o.extend(ff[end:end + 2] + [("mt", 0)])
    second = maxima(1)
    merge(ff[end + 2:], second[:MX_AHEAD])
    main = []
    for g in range(KV):
        for c in range(NT):
            for h in range(GR):
                main.append(("s", g, c, h))
                if g and c == 0 and h in (1, 2):
                    main.append(("ot", g - 1, h - 1))
                if g and (c, h) == (1, 0):
                    main.append(("tr", g - 1))
                if c and h in (2 if c == 1 else 1, 3):
                    main.append(("av", g, c - 1, h // 2 if c > 1 else h - 2))
        main.extend([("av", g, NT - 1, 0), ("av", g, NT - 1, 1)])
    at = 0
    for g in range(KV - 1):
        end = main.index(("s", g, NT - 1, 0))
        merge(main[at:end], maxima(g + 1) if g else second[MX_AHEAD:])
        o.extend(main[end:end + 2] + [("mt", g + 1)])
        at = end + 2
    o.extend(main[at:] + [("ot", KV - 1, 0), ("ot", KV - 1, 1)])
    o.append(("tr", KV - 1))
    o.extend(("at", h, k) for h in range(2) for k in range(KD))
    for t in range(NT):
        o.append(("wo", t))
        if 0 < t < NT - 1:
            o.append(("nb", 3, t - 1))
    return o


def feed_forward_order():
    o = [("x3", h, k) for h in range(2) for k in range(KD)]
    o.append(("b2",))

    def hidden(h, f):
        i = h * NF + f
        return [("h0", h, f)] + ([("hd", i - 1)] if i else []) + [("h", h, f)]

    def result(h, t):
        n = h * TT + t
        return [("w20", h, t), ("w2p", h, t, 1)] + ([("nb", 2, n - 1)] if n else []) + [("w2p", h, t, 2), ("w2", h, t)]

    for f in range(NF):
        o.extend(hidden(0, f))
    for f in range(NF):
        o.extend(hidden(1, f))
        if f in (3, 5, 7):
            o.extend(result(0, (f - 3) // 2))
    o[-4:-4] = [("hd", 2 * NF - 1)]
    o.extend(result(0, 3))
    o[-2:-2] = [("hb",)]
    for t in range(TT):
        o.extend(result(1, t))
        if t == 0:
            o.append(("out", 0))
    o.extend([("nb", 2, 7), ("out", 1)])
    return o


WEIGHT = {"h0": 1.0, "h": 1.0, "w20": 1.0, "w2p": 1.0, "w2": 1.0, "s": 0.7, "av": 1.0, "tr": 0.5}


class Turn(NamedTuple):
    index: object
    part: str


RING = ("xt", "g", "v", "q", "k", "kn", "yt", "w", "x1", "kf", "rv", "x2", "pq", "pk", "pv", "at", "wo", "x3")


def plan_banks(orders):
    late = set(feed_forward_order())
    plans, last, index = {}, {}, {}
    n_late = 0
    for turn, part in enumerate(("first", "loop", "loop", "last")):
        uses = [0] * 8
        before_late = None
        n = n_late if part == "last" else 0
        plan = {}
        for key in orders[part]:
            k = key[0]
            if key in late and before_late is None:
                before_late = list(uses)
                n_late = n
            if k == "a":
                subs = [(key[:3] + (2 * key[3] + j,), [4 + j]) for j in range(2)]
            elif k == "u":
                subs = [(key[:3] + (2 * key[3] + j,), [(n + j) % 4]) for j in range(2)]
                n += 2
            elif k == "o":
                subs = [(key, [6 + key[3]])]
            elif k == "mx":
                subs = [(key, [4 + key[3]])]
            elif k == "mt":
                subs = [(key, [4])]
            elif k == "s":
                subs = [(key, [0, 1] if key[3] % 2 == 0 else [2, 3])]
            elif k == "av":
                subs = [(("ot", key[1]), [6, 7])] if key[2:] == (0, 0) else []
            elif k == "tr":
                subs = [(key + (j,), [6 + j]) for j in range(2)]
            elif k == "h0":
                subs = [(("h",) + key[1:], [n % 4])]
                n += 1
            elif k == "w20":
                subs = [(("w2",) + key[1:], [6 + key[2] % 2])]
            elif k in RING:
                subs = [(key, [n % 4])]
                n += 1
            else:
                subs = []
            for sub, banks in subs:
                before = {(last[x][0], last[x][1] == turn) for x in banks if x in last}
                if part == "loop":
                    index[sub] = (banks, uses[banks[0]])
                plan[sub] = (banks, before)
                for x in banks:
                    last[x] = (sub, turn)
                uses[banks[0]] += 1
        plans[part] = plan
        if part == "loop":
            per_turn, pre = uses, before_late
        elif part == "last":
            late_uses = uses
    for part, plan in plans.items():
        assert all(index[sub][0] == banks for sub, (banks, _) in plan.items())
        plans[part] = {sub: (banks, before, index[sub][1]) for sub, (banks, before) in plan.items()}
    return plans, per_turn, pre, late_uses


def program(nc, A, out):
    NB = A["x"].shape[0]
    order = sequence_order()
    late = [("nb_last", 6), ("nb_last", 7)] + feed_forward_order()
    orders = {"first": [key for key in order if key not in late], "loop": order, "last": late}
    plans, uses, uses_pre, uses_late = plan_banks(orders)
    ctx = ExitStack()
    with ctx:
        def sb(name, shape, dt=F32):
            return ctx.enter_context(nc.sbuf_tensor(name, shape, dt))

        per = {
            "x_in0": 32, "x_in1": 32,
            "init": 2,
            "xt": 4, "x1": 4, "x2": 4, "x3": 4, "at": 4,
            "gz": 8, "gate": 8, "vz": 8,
            "neg": 16, "er": 16, "phi": 16,
            "qs": 8, "kn": 8,
            "am": 32, "state": 28,
            "o_step": 32, "o_div": 16, "y": 16,
            "yt": 8,
            "ln_step": 64, "ln_stat": 32, "ln_eps": 32, "ln_rstd": 32, "ln_done": 32,
            "mix_tmp": 8, "mix": 8, "kr": 4, "ka": 4, "sg": 8, "rv_mul": 8,
            "part1": 6, "rest1": 6, "part2": 6, "parts": 6, "k_out": 16, "q_out": 16,
            "ks": 16 * 6, "qs0": 16 * 12, "qs1": 16 * 6, "qs2": 16 * 6, "v1": 2, "bo": 2,
            "mx": 2 * KV * GR * NT, "nm": KV, "mt1": KV, "mt_r": KV, "mt2": KV, "m_parts": KV,
            "m0": 16 * 6, "m1": 16 * 3, "m2": 16 * 3,
            "p": KV * NT * GR, "o_copy": 2 * KV, "recip": 2 * KV, "div": 2 * KV,
            "fw": 16, "fn": 16, "fr": 16, "sin": 16, "fz": 16, "act": 16, "b2": 2, "out": 32,
        }
        S = {n: ctx.enter_context(nc.semaphore(n)) for n in per}
        filled = [ctx.enter_context(nc.semaphore(f"filled{b}")) for b in range(8)]
        loads = ctx.enter_context(nc.semaphore("constants_loaded"))
        c_pool = ctx.enter_context(nc.semaphore("c_pool"))
        c_act = ctx.enter_context(nc.semaphore("c_act"))
        c_dve = ctx.enter_context(nc.semaphore("c_dve"))

        LATE = {n: (0, per[n]) for n in ("x3", "fw", "fn", "fr", "sin", "fz", "act", "b2", "out")}
        LATE.update({n: (16, 8) for n in ("ln_stat", "ln_eps", "ln_rstd", "ln_done")})
        LATE["ln_step"] = (32, 16)

        def count(b, per_turn, pre, by_late, n):
            if b.part == "first":
                return by_late + n - min(max(n - pre, 0), by_late)
            if b.part == "last":
                return NB * per_turn + n - min(n, pre)
            return b.index * per_turn + n

        def at(b, name, n):
            return count(b, per[name], *LATE.get(name, (0, 0)), n)

        def before(b, name, n):
            return (b.index - 1) * per[name] + n

        w_in = sb("w_in", [P, 4, KD, H0 * DK])
        w_out = sb("w_out", [P, NP0, D])
        w_ffn = sb("w_ffn", [P, 3, KD, D])
        w_q1 = sb("w_q1", [P, KD, D])
        w_vk1 = sb("w_vk1", [P, KD, 2 * KV * HD])
        w_o1 = sb("w_o1", [P, KD, D])
        w_f1 = sb("w_f1", [P, KD, NF * P])
        w_f2 = sb("w_f2", [P, NF, D])
        ident = sb("ident", [P, P])
        decay = sb("decay", [P, H0, P])
        q_pow = sb("q_pow", [P, NP0, P])
        k_pow = sb("k_pow", [P, H0])
        c_pow = sb("c_pow", [P, NP0])
        gate_bias = sb("gate_bias", [P, H0 * DK])
        bo_row = sb("bo_row", [P, D])
        b2_row = sb("b2_row", [P, D])
        bv_row = sb("bv_row", [P, KV * HD])
        cols = sb("cols", [P, 64])
        bq, bk = cols[:, 0:2], cols[0:64, 2:3]
        mu, om = cols[:, 4:8], cols[:, 8:12]
        f_b1, f_turn, f_coef = cols[:, 16:24], cols[:, 24:32], cols[:, 32:40]
        minus_half, ln_eps = cols[:, 40:41], cols[:, 41:42]
        lg_pair = cols[:, 44:48]
        lg = cols[:, 48:56]

        xs = sb("xs", [P, NT, D])
        xf = sb("xf", [P, NT, D])
        r_a = sb("r_a", [P, KD, T + 1])
        x1T, x3T = r_a, r_a
        r_b = sb("r_b", [P, KD * T])
        x0T = r_b[:, 0:KD * HALF].rearrange("p (k n) -> p k n", k=KD)
        x2T = r_b[:, :].rearrange("p (k n) -> p k n", k=KD)
        O_T = r_b[:, 0:T]
        r1 = sb("r1", [P, 8192])
        Qs = r1[:, 0:2048].rearrange("p (a n) -> p a n", a=NP0)
        KT = r1[:, 2048:4096].rearrange("p (a n) -> p a n", a=NP0)
        gate = r1[:, 4096:6144].rearrange("p (t n) -> p t n", t=TT)
        Kn = r1[:, 6144:8192].rearrange("p (c a n) -> p c a n", c=TT, a=NP0)
        probs = r1[:, :].rearrange("p (s n) -> p s n", s=8)
        hidden = r1[:, :].rearrange("p (h f n) -> p h f n", h=2, f=NF)
        r2 = sb("r2", [P, 4096])
        Qbd = r2[:, :].rearrange("p (a e n) -> p a e n", a=NP0, e=2)
        attn = r2[:, 0:NT * D].rearrange("p (t n) -> p t n", t=NT)
        attn_T = r2[:, NT * D:2 * NT * D].rearrange("p (k n) -> p k n", k=KD)
        r3 = sb("r3", [P, TT * NP0 * 3 * WIN])
        Vz = r3[:, :].rearrange("p (t a n) -> p t a n", t=TT, a=NP0)
        q_parts = r3[:, 0:3072].bitcast(BF16).rearrange("p (i m n) -> p i m n", i=3, m=KD)
        r4 = sb("r4", [P, 4096])
        t_exp = r4[:, 0:1024].rearrange("p (s n) -> p s n", s=2)
        t_rel = r4[:, 1024:2048].rearrange("p (s n) -> p s n", s=2)
        Am = r4[:, 2048:3072].rearrange("p (s n) -> p s n", s=4)
        y = r4[:, 3072:4096].rearrange("p (s n) -> p s n", s=2)
        mixed = [r[:, 0:2048].rearrange("p (j k n) -> p j k n", j=2, k=KD) for r in (r4, r3)]
        k_rel = r4[:, 2048:3072].rearrange("p (s n) -> p s n", s=2)
        k_act = r4[:, 3072:4096].rearrange("p (k n) -> p k n", k=KD)
        k_parts = r4[0:64, 0:1536].bitcast(BF16).rearrange("p (i n) -> p i n", i=3)
        f_w = r4[:, 0:1024].rearrange("p (s n) -> p s n", s=2)
        f_n = r4[:, 1024:2048].rearrange("p (s n) -> p s n", s=2)
        f_s = r4[:, 2048:3072].rearrange("p (s n) -> p s n", s=2)
        f_z = r4[:, 3072:4096].rearrange("p (s n) -> p s n", s=2)
        r5 = sb("r5", [P, 1024])
        yT = r5[:, :].rearrange("p (s n) -> p s n", s=2)
        sig = r5[:, 0:512].rearrange("p (s n) -> p s n", s=2)
        prod = r5[:, 512:1024].rearrange("p (s n) -> p s n", s=2)
        rest = r5[:, :].rearrange("p (s n) -> p s n", s=2)
        state = sb("state", [P, 2, NP0, 2 * WIN])
        q_stack = sb("q_stack", [KSTACK, 2, GR, T], BF16)
        q_buf = [q_stack[:, 0], q_stack[:, 1], r3[0:KSTACK, 0:2048].bitcast(BF16).rearrange("p (h n) -> p h n", h=GR)]
        k_stack = sb("k_stack", [KSTACK, KV, T], BF16)
        v_aug = sb("v_aug", [P, NT, KV, 2 * HD])
        neg2 = sb("neg2", [P, GR * NT, 2])
        neg = sb("neg", [P, GR * NT])
        m_parts = sb("m_parts", [32, 3, P], BF16)
        m_rest = sb("m_rest", [32, 2, P])
        recip = sb("recip", [P, 2, TT, GR])
        den = sb("den", [P, 2, 2, 4])
        ln_x = sb("ln_x", [P, 2, D])
        ln_s = sb("ln_s", [P, 2, 16])

        ps = [ctx.enter_context(nc.psum_tensor(f"bank{b}", [P, HALF], F32)) for b in range(4, 8)]
        ps03 = ctx.enter_context(nc.psum_tensor("banks", [P, 4, HALF], F32))
        plan = plans["loop"]
        bank = [ps03[:, i, :] for i in range(4)] + [t[:, :] for t in ps]
        order_of = {}
        for key in order:
            order_of.setdefault(key[0], []).append(key)

        def nth(key):
            return order_of[key[0]].index(key)

        def given_back(key):
            k = key[0]
            if k in ("xt", "x1", "x2", "x3", "at"):
                return k, 2 * key[1] + key[2] + 1
            if k in ("g", "v", "yt", "w", "rv", "kn", "wo", "w2"):
                n = nth(key)
                return {"g": ("gz", n + 1), "v": ("vz", n + 1), "yt": ("yt", TT * key[1] + key[-1] + 1),
                        "w": ("ln_step", 2 * (TT * key[1] + key[-1]) + 1), "rv": ("rv_mul", n + 1), "kn": ("kn", n + 1),
                        "w2": ("ln_step", 2 * (16 + n) + 1), "wo": ("ln_step", 2 * (24 + n) + 1)}[k]
            if k in ("q", "k"):
                return "phi", 2 * (key[1] * NP0 + key[2]) + (k == "k") + 1
            if k in ("a", "u"):
                return {"a": "am", "u": "state"}[k], (key[1] * TT + key[2]) * NP0 + key[3] + 1
            if k == "o":
                return "o_div", nth(key) + 1
            if k == "kf":
                return "kr", 2 * key[1] + key[2] + 1
            if k in ("pq", "pk"):
                return "rest1", 3 * key[1] + (key[2] if k == "pq" else 2) + 1
            if k == "pv":
                return "v1", key[1] + 1
            if k == "mx":
                return "mx", 2 * (key[1] * GR * NT + key[2]) + key[3] + 1
            if k == "mt":
                return "mt_r", key[1] + 1
            if k == "s":
                return "p", (key[1] * NT + key[2]) * GR + key[3] + 1
            if k == "ot":
                return "o_copy", 2 * key[1] + 2
            if k == "tr":
                return "div", 2 * key[1] + key[2] + 1
            assert k == "h"
            return "fz", key[1] * NF + key[2] + 1

        def take(pe, b, key):
            for last, same_turn in plans[b.part][key][1]:
                s, n = given_back(last)
                pe.wait_ge(S[s], at(b, s, n) if same_turn else before(b, s, n))

        def full(eng, b, key):
            banks, _, n = plans[b.part][key]
            x = banks[0]
            eng.wait_ge(filled[x], count(b, uses[x], uses_pre[x], uses_late[x], n + 1))
            return [bank[k] for k in banks]

        def fills(key):
            return filled[plan[key][0][0]]

        def two_heads(window):
            return window.rearrange("p (w n) -> p w n", w=3)[:, 0:3:2, :]

        q_dram = nc.dram_tensor("q_scratch", [3, D, T], BF16).ap()
        k_dram = nc.dram_tensor("k_scratch", [3, KV * HD, T], BF16).ap()
        x_v = A["x"].rearrange("b (t p) d -> b p t d", p=P)
        out_v = out.rearrange("b (t p) d -> b p t d", p=P)

        def ln_index(key):
            if key[0] == "wo":
                return 24 + key[1]
            return {"w": 0, "rv": 8, "w2": 16}[key[0]] + TT * key[1] + key[2]

        block = ctx.enter_context(nc.Block())

        N_LOADS = 30
        N_C_ACT, N_C_DVE = 18, 25

        back, ahead1, left = r4[:, 0:P], r4[:, P:2 * P], r4[:, 2 * P:2 * P + 1]

        def tmp(n):
            return r4[:, 272 + 8 * n:280 + 8 * n]

        @block.sync
        def _(sp):
            def load(dst, src):
                sp.dma_start(dst, src, allow_slow_non_contiguous=True).then_inc(loads, 16)

            for j, n in enumerate(("wq", "wk", "wv", "wg")):
                load(w_in[:, j], A[n].rearrange("(k p) n -> p k n", p=P))
            load(w_out[:], A["wo"].rearrange("(k p) n -> p k n", p=P))
            for j, n in enumerate(("fr", "fk", "fv")):
                load(w_ffn[:, j], A[n].rearrange("(k p) n -> p k n", p=P))
            load(w_q1[:], A["Wq"].rearrange("(k p) n -> p k n", p=P))
            load(w_vk1[:, :, 0:64], A["Wv"].rearrange("(k p) n -> p k n", p=P))
            load(w_vk1[:, :, 64:128], A["Wk"].rearrange("(k p) n -> p k n", p=P))
            load(w_o1[:], A["Wo"].rearrange("(k p) n -> p k n", p=P))
            load(w_f1[:], A["W1"].rearrange("(k p) n -> p k n", p=P))
            load(w_f2[:], A["W2"].rearrange("(k p) n -> p k n", p=P))
            load(gate_bias[:], A["gb"].partition_broadcast(P))
            load(bo_row[:], A["bo"].partition_broadcast(P))
            load(b2_row[:], A["b2"].partition_broadcast(P))
            load(bv_row[:], A["bv"].partition_broadcast(P))
            load(cols[:, 0:2], A["bq"].rearrange("(k p) -> p k", p=P))
            load(cols[0:64, 2:3], A["bk"].rearrange("(k p) -> p k", p=64))
            load(cols[:, 4:6], A["mu_r"].rearrange("(k p) -> p k", p=P))
            load(cols[:, 6:8], A["mu_k"].rearrange("(k p) -> p k", p=P))
            load(f_b1, A["b1"].rearrange("(k p) -> p k", p=P))
            load(f_turn, A["ph"].rearrange("(k p) -> p k", p=P))
            load(f_coef, A["wr"].rearrange("(k p) -> p k", p=P))
            load(tmp(0), A["wi"].rearrange("(k p) -> p k", p=P))
            load(lg, A["dl"].partition_broadcast(P))
            sp.wait_ge(c_pool, 3)
            for i in range(3):
                load(k_stack[96 + i:97 + i, :, :].rearrange("i k n -> i (k n)").rearrange("i (p n) -> i p n", p=32), m_parts[:, i, :])

            def fill_queries(b, g):
                for r, i in enumerate((0, 1, 2, 0, 1, 0)):
                    sp.dma_start(q_buf[g % 3][16 * r:16 * r + 16],
                                 q_dram[i, 64 * g:64 * g + 64, :].rearrange("(h d) n -> d h n", d=HD)).then_inc(S[f"qs{g % 3}"], 16)

            def turn(b):
                if b.part != "last":
                    for i in range(4):
                        if b.part == "loop":
                            sp.wait_ge(S["ln_step"], before(b, "ln_step", 2 * (24 + 2 * i + 1) + 1))
                        sp.dma_start(xs[:, 2 * i:2 * i + 2, :], x_v[b.index][:, 2 * i:2 * i + 2, :]).then_inc(S[f"x_in{i // 2}"], 16)
                for key in orders[b.part]:
                    if key[0] == "stack":
                        sp.wait_ge(S["parts"], at(b, "parts", 6))
                        sp.dma_start(k_dram.rearrange("i p n -> p i n"), k_parts[:, :, :]).then_inc(S["k_out"], 16)
                        sp.dma_start(q_dram.rearrange("i (m p) n -> p i m n", p=P), q_parts[:, :, :, :]).then_inc(S["q_out"], 16)
                        sp.wait_ge(S["k_out"], at(b, "k_out", 16))
                        for r, i in enumerate((0, 0, 0, 1, 1, 2)):
                            sp.dma_start(k_stack[16 * r:16 * r + 16, :, :],
                                         k_dram[i].rearrange("(k d) n -> d k n", d=HD)).then_inc(S["ks"], 16)
                        sp.wait_ge(S["q_out"], at(b, "q_out", 16))
                        for g in range(3):
                            fill_queries(b, g)
                    elif key[0] == "mt":
                        g = key[1]
                        sp.wait_ge(S["m_parts"], at(b, "m_parts", g + 1))
                        for i in range(3):
                            sp.dma_start(q_buf[g % 3][96 + i:97 + i].rearrange("i h n -> i (h n)").rearrange("i (p n) -> i p n", p=32),
                                         m_parts[:, i, :]).then_inc(S[f"m{g % 3}"], 16)
                    elif key[0] == "ot":
                        g = key[1]
                        if g + 3 < KV and key[2] == 0:
                            sp.wait_ge(S["p"], at(b, "p", (g + 1) * NT * GR))
                            fill_queries(b, g + 3)
                    elif key[0] == "out":
                        h = key[1]
                        sp.wait_ge(S["ln_done"], at(b, "ln_done", 16 + TT * (h + 1)))
                        sp.dma_start(out_v[b.index - 1][:, h * TT:(h + 1) * TT, :], xf[:, h * TT:(h + 1) * TT, :]).then_inc(S["out"], 16)

            turn(Turn(0, "first"))
            with sp.Fori(1, NB) as i:
                turn(Turn(i, "loop"))
            turn(Turn(NB, "last"))
            sp.wait_ge(S["out"], at(Turn(NB, "last"), "out", per["out"]))

        @block.gpsimd
        def _(pool):
            g = nc.gpsimd
            g.memset(ident[:], 0.0).then_inc(c_pool, 1)
            g.memset(m_parts[:], 1.0).then_inc(c_pool, 1)
            pool.wait_ge(c_pool, 2)
            g.affine_select(out=ident[:], in_=ident[:], compare_op=ALU.not_equal, fill=1.0, base=0,
                            pattern=[[-1, P]], channel_multiplier=1).then_inc(c_pool, 1)
            g.iota(back, pattern=[[1, P]], base=0, channel_multiplier=-1, allow_small_or_imprecise_dtypes=True).then_inc(c_pool, 1)
            g.iota(ahead1, pattern=[[1, P]], base=1, channel_multiplier=0, allow_small_or_imprecise_dtypes=True).then_inc(c_pool, 1)
            g.iota(left, pattern=[[0, 1]], base=P - 1, channel_multiplier=-1, allow_small_or_imprecise_dtypes=True).then_inc(c_pool, 1)
            g.memset(minus_half, -0.5).then_inc(c_pool, 1)
            g.memset(ln_eps, LN_EPS).then_inc(c_pool, 1)
            g.memset(v_aug[:], 1.0).then_inc(c_pool, 1)
            g.memset(state[:], 0.0).then_inc(c_pool, 1)
            g.memset(r_a[:, :, 0:1], 0.0).then_inc(c_pool, 1)
            pool.wait_ge(c_act, 2 + H0)
            g.affine_select(out=decay[:], in_=decay[:], compare_op=ALU.is_ge, fill=0.0, base=0,
                            pattern=[[0, H0], [1, P]], channel_multiplier=-1).then_inc(c_pool, 1)
            pool.wait_ge(c_act, N_C_ACT)
            pool.wait_ge(c_dve, N_C_DVE)
            for name, (_, n) in LATE.items():
                g.sem_inc(S[name], n)
            for x, n in enumerate(uses_late):
                if n:
                    g.sem_inc(filled[x], n)

            def turn(b):
                for key in orders[b.part]:
                    k = key[0]
                    if k == "init":
                        g.memset(r2[:], 0.0).then_inc(S["init"], 1)
                        g.memset(r3[:, :].rearrange("p (t n) -> p t n", n=3 * WIN)[:, :, WIN:2 * WIN], 0.0)
                        g.memset(r3[:, :].rearrange("p (t n) -> p t n", n=3 * WIN)[:, :, DK:DK + 1], 1.0)
                        g.memset(r3[:, :].rearrange("p (t n) -> p t n", n=3 * WIN)[:, :, 3 * WIN - 1:3 * WIN],
                                 1.0).then_inc(S["init"], 1)
                    elif k == "o":
                        _, h, c, pp = key
                        pool.wait_ge(S["o_div"], at(b, "o_div", nth(key) + 1))
                        pool.wait_ge(S["gate"], at(b, "gate", h * TT + c + 1))
                        ys = y[:, c % 2, 256 * pp:256 * pp + 256]
                        g.tensor_tensor(ys, ys, gate[:, c, 256 * pp:256 * pp + 256], ALU.mult).then_inc(S["y"], 1)
                    elif k in ("w", "rv", "wo", "w2"):
                        n = ln_index(key)
                        pool.wait_ge(S["ln_stat"], at(b, "ln_stat", n + 1))
                        v = ln_s[:, n % 2, 9:10]
                        g.tensor_tensor(v, ln_s[:, n % 2, 7:8], ln_eps, ALU.add).then_inc(S["ln_eps"], 1)
                        pool.wait_ge(S["ln_eps"], at(b, "ln_eps", n + 1))
                        g.tensor_tensor(ln_s[:, n % 2, 8:9], v, minus_half, ALU.pow).then_inc(S["ln_rstd"], 1)
                    elif k == "bo":
                        h = key[1]
                        pool.wait_ge(S["x2"], at(b, "x2", 2 * h + 2))
                        g.tensor_tensor(xs[:, h * TT:(h + 1) * TT, :], xs[:, h * TT:(h + 1) * TT, :],
                                        bo_row[:, :].unsqueeze(1).to_broadcast([P, TT, D]), ALU.add).then_inc(S["bo"], 1)
                    elif k == "b2":
                        pool.wait_ge(S["x3"], at(b, "x3", 4))
                        for h in range(2):
                            g.tensor_tensor(xf[:, h * TT:(h + 1) * TT, :], xf[:, h * TT:(h + 1) * TT, :],
                                            b2_row[:, :].unsqueeze(1).to_broadcast([P, TT, D]), ALU.add).then_inc(S["b2"], 1)
                    elif k == "h":
                        i = nth(key)
                        pool.wait_ge(S["fn"], at(b, "fn", i + 1))
                        g.tensor_tensor(f_n[:, i % 2, :], f_w[:, i % 2, :], f_n[:, i % 2, :], ALU.subtract).then_inc(S["fr"], 1)

            turn(Turn(0, "first"))
            with pool.Fori(1, NB) as i:
                turn(Turn(i, "loop"))
            turn(Turn(NB, "last"))

        @block.scalar
        def _(act):
            a = nc.scalar.activation
            act.wait_ge(loads, 16 * N_LOADS)
            act.wait_ge(c_dve, 2)
            a(tmp(3), tmp(2), ACT.Exp, scale=-1.0).then_inc(c_act, 1)
            act.wait_ge(c_act, 1)
            a(tmp(4), tmp(3), ACT.Ln, bias=1.0).then_inc(c_act, 1)
            act.wait_ge(c_dve, 8)
            act.wait_ge(c_pool, 6)
            for h in range(H0):
                a(decay[:, h, :], back, ACT.Exp, scale=lg[:, h:h + 1]).then_inc(c_act, 1)
            for p in range(NP0):
                a(q_pow[:, p, :], ahead1, ACT.Exp, scale=lg_pair[:, p:p + 1]).then_inc(c_act, 1)
            a(c_pow[:], lg_pair, ACT.Exp, scale=float(P)).then_inc(c_act, 1)
            a(k_pow[:], lg, ACT.Exp, scale=left).then_inc(c_act, 1)
            act.wait_ge(c_dve, 20)
            a(tmp(5), tmp(9), ACT.Sin, scale=TURN).then_inc(c_act, 1)
            a(tmp(6), tmp(10), ACT.Sin, scale=TURN).then_inc(c_act, 1)

            def turn(b):
                def relu(i):
                    h, f = i // NF, i % NF
                    act.wait_ge(S["fz"], at(b, "fz", i + 1))
                    a(hidden[:, h, f, :], f_z[:, i % 2, :], ACT.Relu, bias=f_b1[:, f:f + 1]).then_inc(S["act"], 1)

                for key in orders[b.part]:
                    k = key[0]
                    if k in ("xt", "x1", "x2", "x3", "at"):
                        _, h, kd = key
                        dst = {"xt": x0T[:, kd, :], "x1": x1T[:, kd, 1 + h * HALF:1 + (h + 1) * HALF],
                               "x2": x2T[:, kd, h * HALF:(h + 1) * HALF],
                               "at": attn_T[:, kd, h * HALF:(h + 1) * HALF],
                               "x3": x3T[:, kd, 1 + h * HALF:1 + (h + 1) * HALF]}[k]
                        (src,) = full(act, b, key)
                        a(dst, src, ACT.Copy).then_inc(S[k], 1)
                    elif k == "sg":
                        for t in range(TT):
                            act.wait_ge(S["gz"], at(b, "gz", key[1] * TT + t + 1))
                            a(gate[:, t, :], gate[:, t, :], ACT.Sigmoid).then_inc(S["gate"], 1)
                    elif k == "v":
                        _, h, t = key
                        (src,) = full(act, b, key)
                        if t == 0 and h == 0:
                            act.wait_ge(S["init"], at(b, "init", 2))
                        a(Vz[:, t].rearrange("p a n -> p (a n)").rearrange("p (e n) -> p e n", n=WIN * 3)[:, :, 0:DK],
                          src.rearrange("p (a e n) -> p a e n", a=NP0, e=2)[:, :, 0, :], ACT.Copy)
                        a(Vz[:, t].rearrange("p a n -> p (a n)").rearrange("p (e n) -> p e n", n=WIN * 3)[:, :, 2 * WIN:2 * WIN + DK],
                          src.rearrange("p (a e n) -> p a e n", a=NP0, e=2)[:, :, 1, :], ACT.Copy).then_inc(S["vz"], 1)
                    elif k in ("q", "k"):
                        _, h, p = key
                        i = 2 * (h * NP0 + p) + (k == "k")
                        (src,) = full(act, b, key)
                        if i >= 2:
                            act.wait_ge(S["phi"], at(b, "phi", i - 1))
                        a(t_rel[:, i % 2, :], src, ACT.Relu, scale=-1.0).then_inc(S["neg"], 1)
                        act.wait_ge(S["neg"], at(b, "neg", i + 1))
                        a(t_exp[:, i % 2, :], t_rel[:, i % 2, :], ACT.Exp, scale=-1.0).then_inc(S["er"], 1)
                    elif k == "yt":
                        _, h, c = key
                        (src,) = full(act, b, key)
                        a(yT[:, c % 2, :], src, ACT.Copy).then_inc(S["yt"], 1)
                    elif k == "mix":
                        _, h, j = key
                        if j == 0:
                            act.wait_ge(S["x1"], at(b, "x1", 2 * h + 2))
                        if (h, j) == (0, 0):
                            act.wait_ge(S["phi"], at(b, "phi", per["phi"]))
                        a(mixed[h][:, j // 2, j % 2, :], x1T[:, j % 2, h * HALF:(h + 1) * HALF], ACT.Copy,
                          scale=om[:, j:j + 1]).then_inc(S["mix_tmp"], 1)
                    elif k == "kf":
                        _, h, m = key
                        i = 2 * h + m
                        (src,) = full(act, b, key)
                        a(k_rel[:, m, :], src, ACT.Relu).then_inc(S["kr"], 1)
                        act.wait_ge(S["kr"], at(b, "kr", i + 1))
                        a(k_act[:, m, :], k_rel[:, m, :], ACT.Square).then_inc(S["ka"], 1)
                    elif k == "rv":
                        _, h, t = key
                        (src,) = full(act, b, key)
                        n = h * TT + t
                        if n >= 2:
                            act.wait_ge(S["rv_mul"], at(b, "rv_mul", n - 1))
                        a(sig[:, t % 2, :], src[:, 0:D], ACT.Sigmoid).then_inc(S["sg"], 1)
                    elif k == "pq":
                        _, h, m = key
                        (src,) = full(act, b, key)
                        a(q_parts[:, 0, m, h * HALF:(h + 1) * HALF], src, ACT.Identity, bias=bq[:, m:m + 1]).then_inc(S["part1"], 1)
                    elif k == "pk":
                        h = key[1]
                        (src,) = full(act, b, key)
                        a(k_parts[:, 0, h * HALF:(h + 1) * HALF], src[0:64, :], ACT.Identity, bias=bk).then_inc(S["part1"], 1)
                    elif k == "mt":
                        g = key[1]
                        (src,) = full(act, b, key)
                        if g:
                            act.wait_ge(S[f"m{(g - 1) % 3}"], at(b, f"m{(g - 1) % 3}", 48 * (1 + (g - 1) // 3)))
                        a(m_parts[:, 0, :], src[0:32, 0:P], ACT.Copy).then_inc(S["mt1"], 1)
                    elif k == "s":
                        _, g, c, h = key
                        full(act, b, key)
                        lo = 0 if h % 2 == 0 else 2
                        a(probs[:, 4 * (c % 2) + h, :], ps03[:, lo:lo + 2, :].rearrange("p a n -> p (a n)"), ACT.Exp,
                          scale=1.0 / HD ** 0.5).then_inc(S["p"], 1)
                    elif k == "ot":
                        g = key[1]
                        src = full(act, b, key[:2])
                        j = key[2]
                        if g and j == 0:
                            act.wait_ge(S["div"], at(b, "div", 2 * g))
                        a(O_T[:, j * HALF:(j + 1) * HALF], src[j], ACT.Copy).then_inc(S["o_copy"], 1)
                    elif k in ("h", "hb"):
                        i = nth(key) if k == "h" else 2 * NF
                        if k == "h":
                            f = key[2]
                            (src,) = full(act, b, key)
                            if i == 0 and b.part == "loop":
                                act.wait_ge(S["k_out"], at(b, "k_out", 16))
                            if i >= 2:
                                act.wait_ge(S["fr"], at(b, "fr", i - 1))
                            a(f_w[:, i % 2, :], src, ACT.Identity, bias=f_turn[:, f:f + 1], scale=0.1 / TWO_PI).then_inc(S["fw"], 1)
                        if i >= 2:
                            relu(i - 2)
                        if i:
                            i -= 1
                            act.wait_ge(S["fr"], at(b, "fr", i + 1))
                            if i >= 2:
                                act.wait_ge(S["fz"], at(b, "fz", i - 1))
                            a(f_s[:, i % 2, :], f_n[:, i % 2, :], ACT.Sin, scale=TURN).then_inc(S["sin"], 1)
                        if k == "hb":
                            relu(i)

            turn(Turn(0, "first"))
            with act.Fori(1, NB) as i:
                turn(Turn(i, "loop"))
            turn(Turn(NB, "last"))

        @block.vector
        def _(dve):
            v = nc.vector
            steps = [0]

            def then(ins):
                steps[0] += 1
                ins.then_inc(c_dve, 1)
                dve.wait_ge(c_dve, steps[0])

            dve.wait_ge(loads, 16 * N_LOADS)
            then(v.tensor_scalar(tmp(1), lg, -1.0, None, ALU.mult))
            then(v.tensor_tensor(tmp(2), tmp(1), lg, ALU.max))
            then(v.tensor_scalar(tmp(1), lg, 0.0, None, ALU.min))
            dve.wait_ge(c_act, 2)
            then(v.tensor_tensor(lg, tmp(1), tmp(4), ALU.subtract))
            then(v.tensor_copy(lg_pair[0:64], lg[0:64, 0:H0:2]))
            then(v.tensor_copy(lg_pair[64:128], lg[64:128, 1:H0:2]))
            dve.wait_ge(c_pool, 4)
            then(v.tensor_scalar(back, back, 0.0, None, ALU.max))
            then(v.tensor_scalar(om, mu, -1.0, 1.0, ALU.mult, ALU.add))
            then(v.tensor_scalar(tmp(7), f_turn, 1.0 / TWO_PI, MAGIC, ALU.mult, ALU.add))
            then(v.tensor_scalar(tmp(7), tmp(7), MAGIC, None, ALU.subtract))
            for part in (PI_A, PI_B, PI_C):
                then(v.scalar_tensor_tensor(f_turn, tmp(7), -part, f_turn, ALU.mult, ALU.add))
            then(v.tensor_scalar(f_turn, f_turn, 1.0 / TWO_PI, None, ALU.mult))
            then(v.tensor_scalar(tmp(8), f_turn, MAGIC, MAGIC, ALU.add, ALU.subtract))
            then(v.tensor_tensor(tmp(9), f_turn, tmp(8), ALU.subtract))
            then(v.tensor_scalar(tmp(10), f_turn, 0.25, None, ALU.add))
            then(v.tensor_scalar(tmp(8), tmp(10), MAGIC, MAGIC, ALU.add, ALU.subtract))
            then(v.tensor_tensor(tmp(10), tmp(10), tmp(8), ALU.subtract))
            then(v.scalar_tensor_tensor(f_turn, f_b1, 0.1 / TWO_PI, f_turn, ALU.mult, ALU.add))
            dve.wait_ge(c_act, N_C_ACT)
            then(v.tensor_tensor(tmp(6), tmp(6), f_coef, ALU.mult))
            then(v.tensor_tensor(tmp(5), tmp(5), tmp(0), ALU.mult))
            then(v.tensor_tensor(tmp(5), tmp(5), tmp(6), ALU.add))
            then(v.tensor_tensor(tmp(5), tmp(5), tmp(0), ALU.mult))
            then(v.tensor_scalar(f_coef, tmp(5), 0.1, None, ALU.mult))
            dve.wait_ge(c_pool, 12)

            def norm_stats(b, n, psum, resid, key):
                xs, st = ln_x[:, n % 2, :], ln_s[:, n % 2, :]
                if n >= 2:
                    dve.wait_ge(S["ln_done"], at(b, "ln_done", n - 1))
                elif b.part == "loop":
                    dve.wait_ge(S["ln_done"], before(b, "ln_done", per["ln_done"] + n - 1))
                v.tensor_tensor(xs, resid, psum, ALU.add).then_inc(S["ln_step"], 1)
                dve.wait_ge(S["ln_step"], at(b, "ln_step", 2 * n + 1))
                v.bn_stats(st[:, 0:6], xs).then_inc(S["ln_step"], 1)
                dve.wait_ge(S["ln_step"], at(b, "ln_step", 2 * n + 2))
                v.memset(st[:, 10:11], 0.0)
                v.bn_aggr(st[:, 6:8], st[:, 0:6]).then_inc(S["ln_stat"], 1)

            def turn(b):
                for key in orders[b.part]:
                    k = key[0]
                    if k == "g":
                        _, h, t = key
                        (src,) = full(dve, b, key)
                        if h:
                            dve.wait_ge(S["y"], at(b, "y", 2 * (t + 1)))
                        v.tensor_tensor(gate[:, t, :], src, gate_bias[:], ALU.add).then_inc(S["gz"], 1)
                    elif k in ("q", "k"):
                        _, h, p = key
                        i = 2 * (h * NP0 + p) + (k == "k")
                        (src,) = full(dve, b, key)
                        dve.wait_ge(S["er"], at(b, "er", i + 1))
                        if k == "k":
                            v.scalar_tensor_tensor(KT[:, p, :], src, 0.0, t_exp[:, i % 2, :], ALU.max, ALU.add).then_inc(S["phi"], 1)
                        else:
                            if i == 0:
                                dve.wait_ge(S["init"], at(b, "init", 1))
                            v.scalar_tensor_tensor(Qbd[0:64, p, 0, :], src[0:64], 0.0, t_exp[0:64, i % 2, :],
                                                   ALU.max, ALU.add)
                            v.scalar_tensor_tensor(Qbd[64:128, p, 1, :], src[64:128], 0.0, t_exp[64:128, i % 2, :],
                                                   ALU.max, ALU.add).then_inc(S["phi"], 1)
                            dve.wait_ge(S["phi"], at(b, "phi", i + 1))
                            for e in range(2):
                                rows = slice(64 * e, 64 * e + 64)
                                last = v.tensor_tensor(Qs[rows, p, :].rearrange("p (c n) -> p c n", c=TT),
                                                       Qbd[rows, p, e, :].rearrange("p (c n) -> p c n", c=TT),
                                                       q_pow[rows, p, :].unsqueeze(1).to_broadcast([64, TT, P]), ALU.mult)
                            last.then_inc(S["qs"], 1)
                    elif k == "kn":
                        _, h, p = key
                        (src,) = full(dve, b, key)
                        v.tensor_tensor(Kn[:, :, p, :].rearrange("p c (e n) -> p c e n", e=2),
                                        src.rearrange("p (c e n) -> p c e n", c=TT, e=2),
                                        k_pow[:, 2 * p:2 * p + 2].unsqueeze(1).unsqueeze(3).to_broadcast([P, TT, 2, DK]),
                                        ALU.mult).then_inc(S["kn"], 1)
                    elif k == "a":
                        _, h, c, pp = key
                        for j in range(2):
                            p = 2 * pp + j
                            sub = ("a", h, c, p)
                            (src,) = full(dve, b, sub)
                            v.tensor_tensor(Am[:, p, :], src[:, 0:2 * P],
                                            decay[:, 2 * p:2 * p + 2, :].rearrange("p e n -> p (e n)"), ALU.mult).then_inc(S["am"], 1)
                    elif k == "u":
                        _, h, c, pp = key
                        for j in range(2):
                            p = 2 * pp + j
                            (src,) = full(dve, b, ("u", h, c, p))
                            now, new = c % 2, (c + 1) % 2
                            for e in range(2):
                                rows, cs = slice(64 * e, 64 * e + 64), slice(WIN * e, WIN * e + WIN)
                                if (h, c) == (0, 0):
                                    last = v.tensor_copy(state[rows, new, p, cs], src[rows, cs])
                                else:
                                    if e == 0:
                                        dve.wait_ge(S["state"], at(b, "state", (h * TT + c - 1) * NP0 + p + 1))
                                    last = v.scalar_tensor_tensor(state[rows, new, p, cs], state[rows, now, p, cs],
                                                                  c_pow[rows, p:p + 1], src[rows, cs], ALU.mult, ALU.add)
                            last.then_inc(S["state"], 1)
                    elif k == "o":
                        _, h, c, pp = key
                        n = nth(key)
                        (src,) = full(dve, b, key)
                        heads = src[:, 0:4 * WIN].rearrange("p (e n) -> p e n", n=WIN)
                        v.tensor_scalar(den[:, n % 2, 0, :], heads[:, :, DK], DEN_EPS, None, ALU.add).then_inc(S["o_step"], 1)
                        dve.wait_ge(S["o_step"], at(b, "o_step", 2 * n + 1))
                        v.reciprocal(den[:, n % 2, 1, :], den[:, n % 2, 0, :]).then_inc(S["o_step"], 1)
                        dve.wait_ge(S["o_step"], at(b, "o_step", 2 * n + 2))
                        v.tensor_tensor(y[:, c % 2, 256 * pp:256 * pp + 256].rearrange("p (e n) -> p e n", e=4), heads[:, :, 0:DK],
                                        den[:, n % 2, 1, :].unsqueeze(2).to_broadcast([P, 4, DK]), ALU.mult).then_inc(S["o_div"], 1)
                    elif k == "w":
                        _, h, c = key
                        t = h * TT + c
                        (src,) = full(dve, b, key)
                        norm_stats(b, t, src[:, 0:D], xs[:, t, :], key)
                    elif k == "mix":
                        _, h, j = key
                        dve.wait_ge(S["mix_tmp"], at(b, "mix_tmp", 4 * h + j + 1))
                        m = mixed[h][:, j // 2, j % 2, :]
                        v.scalar_tensor_tensor(m, x1T[:, j % 2, 1 + h * HALF:1 + (h + 1) * HALF],
                                               mu[:, j:j + 1], m, ALU.mult, ALU.add).then_inc(S["mix"], 1)
                    elif k == "rv":
                        _, h, t = key
                        n = h * TT + t
                        dve.wait_ge(S["sg"], at(b, "sg", n + 1))
                        (src,) = full(dve, b, key)
                        if n >= 2:
                            dve.wait_ge(S["ln_step"], at(b, "ln_step", 2 * (8 + n - 2) + 1))
                        v.tensor_tensor(prod[:, t % 2, :], sig[:, t % 2, :], src[:, D:2 * D], ALU.mult).then_inc(S["rv_mul"], 1)
                        dve.wait_ge(S["rv_mul"], at(b, "rv_mul", n + 1))
                        norm_stats(b, 8 + n, prod[:, t % 2, :], xs[:, n, :], key)
                    elif k in ("pq", "pk"):
                        i = 3 * key[1] + (key[2] if k == "pq" else 2)
                        (src,) = full(dve, b, key)
                        h = key[1]
                        cut = slice(h * HALF, (h + 1) * HALF)
                        if k == "pq":
                            m = key[2]
                            bias, left_over = bq[:, m:m + 1], rest[:, i % 2, :]
                            parts = [q_parts[:, j, m, cut] for j in range(3)]
                        else:
                            src, bias, parts, left_over = src[0:64], bk, [k_parts[:, j, cut] for j in range(3)], rest[0:64, i % 2, :]
                        dve.wait_ge(S["part1"], at(b, "part1", i + 1))
                        v.scalar_tensor_tensor(left_over, src, bias, parts[0], ALU.add, ALU.subtract).then_inc(S["rest1"], 1)
                        dve.wait_ge(S["rest1"], at(b, "rest1", i + 1))
                        v.tensor_copy(parts[1], left_over).then_inc(S["part2"], 1)
                        dve.wait_ge(S["part2"], at(b, "part2", i + 1))
                        v.tensor_tensor(parts[2], left_over, parts[1], ALU.subtract).then_inc(S["parts"], 1)
                    elif k == "pv":
                        h = key[1]
                        (src,) = full(dve, b, key)
                        v.tensor_tensor(v_aug[:, h * TT:(h + 1) * TT, :, 0:HD],
                                        src.rearrange("p (t n) -> p t n", t=TT)[:, :, 0:KV * HD].rearrange("p t (k d) -> p t k d", k=KV),
                                        bv_row[:, :].rearrange("p (k d) -> p k d", k=KV).unsqueeze(1).to_broadcast([P, TT, KV, HD]),
                                        ALU.add).then_inc(S["v1"], 1)
                    elif k == "mx":
                        _, g, n, j = key
                        (src,) = full(dve, b, key)
                        if g and (n, j) == (0, 0):
                            dve.wait_ge(S["nm"], at(b, "nm", g))
                        v.tensor_reduce(neg2[:, n, j:j + 1], src, AX.X, ALU.max, negate=True).then_inc(S["mx"], 1)
                        if (n, j) == (GR * NT - 1, 1):
                            dve.wait_ge(S["mx"], at(b, "mx", 2 * (g + 1) * GR * NT))
                            v.tensor_tensor(neg[:], neg2[:, :, 0], neg2[:, :, 1], ALU.min).then_inc(S["nm"], 1)
                    elif k == "mt":
                        g = key[1]
                        (src,) = full(dve, b, key)
                        m_rest1, m_rest2 = m_rest[:, 0, :], m_rest[:, 1, :]
                        dve.wait_ge(S["mt1"], at(b, "mt1", g + 1))
                        v.tensor_tensor(m_rest1, src[0:32, 0:P], m_parts[:, 0, :], ALU.subtract).then_inc(S["mt_r"], 1)
                        dve.wait_ge(S["mt_r"], at(b, "mt_r", g + 1))
                        v.tensor_copy(m_parts[:, 1, :], m_rest1).then_inc(S["mt2"], 1)
                        dve.wait_ge(S["mt2"], at(b, "mt2", g + 1))
                        v.tensor_tensor(m_parts[:, 2, :], m_rest1, m_parts[:, 1, :], ALU.subtract).then_inc(S["m_parts"], 1)
                    elif k == "tr":
                        g = key[1]
                        for j in range(2):
                            (src,) = full(dve, b, key + (j,))
                            heads = src.rearrange("p (t h n) -> p t h n", t=TT, h=GR)
                            v.reciprocal(recip[:, j], heads[:, :, :, HD]).then_inc(S["recip"], 1)
                            dve.wait_ge(S["recip"], at(b, "recip", 2 * g + j + 1))
                            v.tensor_tensor(attn[:, j * TT:(j + 1) * TT, :].rearrange("p t (h k d) -> p t h k d", h=GR, k=KV)[:, :, :, g, :],
                                            heads[:, :, :, 0:HD], recip[:, j].unsqueeze(3).to_broadcast([P, TT, GR, HD]),
                                            ALU.mult).then_inc(S["div"], 1)
                    elif k == "wo":
                        t = key[1]
                        if t % TT == 0:
                            dve.wait_ge(S["bo"], at(b, "bo", t // TT + 1))
                        (src,) = full(dve, b, key)
                        norm_stats(b, 24 + t, src[:, 0:D], xs[:, t, :], key)
                    elif k in ("hd", "hb"):
                        i = key[1] if k == "hd" else 2 * NF
                        if k == "hd":
                            dve.wait_ge(S["fw"], at(b, "fw", i + 1))
                            if i >= 2:
                                dve.wait_ge(S["sin"], at(b, "sin", i - 1))
                            v.tensor_scalar(f_n[:, i % 2, :], f_w[:, i % 2, :], MAGIC, MAGIC, ALU.add, ALU.subtract).then_inc(S["fn"], 1)
                        if i:
                            i -= 1
                            h, f = i // NF, i % NF
                            dve.wait_ge(S["sin"], at(b, "sin", i + 1))
                            (src,) = full(dve, b, ("h", h, f))
                            if i >= 2:
                                dve.wait_ge(S["act"], at(b, "act", i - 1))
                            v.scalar_tensor_tensor(f_z[:, i % 2, :], f_s[:, i % 2, :], f_coef[:, f:f + 1], src,
                                                   ALU.mult, ALU.add).then_inc(S["fz"], 1)
                    elif k == "w2":
                        _, h, t = key
                        n = h * TT + t
                        if t == 0:
                            dve.wait_ge(S["b2"], at(b, "b2", h + 1))
                        (src,) = full(dve, b, key)
                        norm_stats(b, 16 + n, src[:, 0:D], xf[:, n, :], key)
                    elif k == "nb_last":
                        t = key[1]
                        dve.wait_ge(S["ln_rstd"], before(b, "ln_rstd", 24 + t + 1))
                        v.tensor_scalar(xf[:, t, :], ln_x[:, t % 2, :], ln_s[:, t % 2, 6:7], ln_s[:, t % 2, 8:9],
                                        ALU.subtract, ALU.mult).then_inc(S["ln_done"], 1)
                    elif k == "nb":
                        n = 8 * key[1] + key[2]
                        dve.wait_ge(S["ln_rstd"], at(b, "ln_rstd", n + 1))
                        if key == ("nb", 3, 0) and b.part == "loop":
                            dve.wait_ge(S["out"], at(b, "out", per["out"]))
                        v.tensor_scalar((xs if key[1] < 2 else xf)[:, n % 8, :], ln_x[:, n % 2, :], ln_s[:, n % 2, 6:7], ln_s[:, n % 2, 8:9],
                                        ALU.subtract, ALU.mult).then_inc(S["ln_done"], 1)

            turn(Turn(0, "first"))
            with dve.Fori(1, NB) as i:
                turn(Turn(i, "loop"))
            turn(Turn(NB, "last"))

        @block.tensor
        def _(pe):
            mm = nc.tensor.matmul

            def product(dst, terms):
                for i, (lhsT, rhs) in enumerate(terms):
                    last = mm(dst, lhsT, rhs, start=(i == 0), stop=(i == len(terms) - 1))
                return last

            def flip(key, tiles):
                (o,) = [bank[k] for k in plan[key][0]]
                for i, t in enumerate(tiles):
                    last = nc.tensor.transpose(o[0:t.shape[1], i * P:i * P + t.shape[0]], t, ident[:])
                last.then_inc(fills(key), 1)

            pe.wait_ge(c_pool, 12)
            pe.wait_ge(c_dve, N_C_DVE)
            def turn(b):
                for key in orders[b.part]:
                    k = key[0]
                    if k == "xt":
                        _, h, kd = key
                        if kd == 0:
                            pe.wait_ge(S[f"x_in{h}"], at(b, f"x_in{h}", 32))
                        take(pe, b, key)
                        flip(key, [xs[:, h * TT + t, kd * P:(kd + 1) * P] for t in range(TT)])
                    elif k == "x3":
                        _, h, kd = key
                        if kd == 0:
                            pe.wait_ge(S["ln_done"], before(b, "ln_done", 24 + TT * (h + 1)))
                        take(pe, b, key)
                        flip(key, [xf[:, h * TT + t, kd * P:(kd + 1) * P] for t in range(TT)])
                    elif k in ("x1", "x2"):
                        _, h, kd = key
                        pe.wait_ge(S["ln_done"], at(b, "ln_done", (0 if k == "x1" else 8) + TT * (h + 1)))
                        take(pe, b, key)
                        flip(key, [xs[:, h * TT + t, kd * P:(kd + 1) * P] for t in range(TT)])
                    elif k == "tr":
                        for j in range(2):
                            pe.wait_ge(S["o_copy"], at(b, "o_copy", 2 * key[1] + j + 1))
                            take(pe, b, key + (j,))
                            flip(key + (j,), [O_T[:, t * P:(t + 1) * P] for t in range(j * TT, (j + 1) * TT)])
                    elif k == "at":
                        _, h, kd = key
                        pe.wait_ge(S["div"], at(b, "div", 2 * (KV - 1) + h + 1))
                        take(pe, b, key)
                        flip(key, [attn[:, h * TT + t, kd * P:(kd + 1) * P] for t in range(TT)])
                    elif k in ("g", "v"):
                        _, h, t = key
                        take(pe, b, key)
                        w = w_in[:, 3 if k == "g" else 2]
                        product(bank[plan[key][0][0]], [(x0T[:, kd, t * P:(t + 1) * P], w[:, kd, :]) for kd in range(KD)])\
                            .then_inc(fills(key), 1)
                    elif k in ("q", "k"):
                        _, h, p = key
                        if p == 0:
                            pe.wait_ge(S["xt"], at(b, "xt", 2 * h + 2))
                        take(pe, b, key)
                        w = w_in[:, 0 if k == "q" else 1]
                        product(bank[plan[key][0][0]], [(w[:, kd, p * P:(p + 1) * P], x0T[:, kd, :]) for kd in range(KD)])\
                            .then_inc(fills(key), 1)
                    elif k == "kn":
                        _, h, p = key
                        pe.wait_ge(S["phi"], at(b, "phi", 2 * (h * NP0 + p) + 2))
                        take(pe, b, key)
                        flip(key, [KT[:, p, c * P:(c + 1) * P] for c in range(TT)])
                    elif k == "a":
                        _, h, c, pp = key
                        for j in range(2):
                            p = 2 * pp + j
                            sub = ("a", h, c, p)
                            if c == 0:
                                pe.wait_ge(S["phi"], at(b, "phi", 2 * (h * NP0 + p) + 2))
                            take(pe, b, sub)
                            product(bank[plan[sub][0][0]][:, 0:2 * P].rearrange("p (e n) -> p e n", e=2),
                                    [(KT[:, p, c * P:(c + 1) * P], Qbd[:, p, :, c * P:(c + 1) * P])]).then_inc(fills(sub), 1)
                    elif k == "u":
                        _, h, c, pp = key
                        for j in range(2):
                            p = 2 * pp + j
                            sub = ("u", h, c, p)
                            if c == 0:
                                pe.wait_ge(S["kn"], at(b, "kn", h * NP0 + p + 1))
                                pe.wait_ge(S["vz"], at(b, "vz", (h + 1) * TT))
                            take(pe, b, sub)
                            product(bank[plan[sub][0][0]][:, 0:2 * WIN].rearrange("p (w n) -> p w n", w=2),
                                    [(Kn[:, c, p, :], two_heads(Vz[:, c, p, :]))]).then_inc(fills(sub), 1)
                    elif k == "o":
                        _, h, c, pp = key
                        take(pe, b, key)
                        o = bank[plan[key][0][0]]
                        if pp == 0:
                            pe.wait_ge(S["vz"], at(b, "vz", h * TT + c + 1))
                        for j in range(2):
                            p = 2 * pp + j
                            pe.wait_ge(S["am"], at(b, "am", (h * TT + c) * NP0 + p + 1))
                            terms = [(Am[:, p, e * P:(e + 1) * P], Vz[:, c, p, e * WIN:(e + 2) * WIN]) for e in range(2)]
                            if (h, c) != (0, 0):
                                if c == 0:
                                    pe.wait_ge(S["qs"], at(b, "qs", h * NP0 + p + 1))
                                pe.wait_ge(S["state"], at(b, "state", (h * TT + c - 1) * NP0 + p + 1))
                                terms.append((Qs[:, p, c * P:(c + 1) * P], state[:, c % 2, p, :]))
                            last = product(o[:, j * 2 * WIN:(j + 1) * 2 * WIN], terms)
                        last.then_inc(fills(key), 1)
                    elif k == "yt":
                        _, h, c = key
                        pe.wait_ge(S["y"], at(b, "y", 2 * (h * TT + c + 1)))
                        take(pe, b, key)
                        flip(key, [y[:, c % 2, f * P:(f + 1) * P] for f in range(4)])
                    elif k == "w":
                        _, h, c = key
                        pe.wait_ge(S["yt"], at(b, "yt", h * TT + c + 1))
                        take(pe, b, key)
                        product(bank[plan[key][0][0]][:, 0:D],
                                [(yT[:, c % 2, f * P:(f + 1) * P], w_out[:, f, :]) for f in range(4)]).then_inc(fills(key), 1)
                    elif k == "kf":
                        _, h, m = key
                        pe.wait_ge(S["mix"], at(b, "mix", 4 * h + 4))
                        take(pe, b, key)
                        product(bank[plan[key][0][0]],
                                [(w_ffn[:, 1, kd, m * P:(m + 1) * P], mixed[h][:, 1, kd, :]) for kd in range(KD)]).then_inc(fills(key), 1)
                    elif k == "rv":
                        _, h, t = key
                        take(pe, b, key)
                        o = bank[plan[key][0][0]]
                        ts = slice(t * P, (t + 1) * P)
                        product(o[:, 0:D], [(mixed[h][:, 0, kd, ts], w_ffn[:, 0, kd, :]) for kd in range(KD)])
                        if t == 0:
                            pe.wait_ge(S["ka"], at(b, "ka", 2 * h + 2))
                        product(o[:, D:2 * D], [(k_act[:, kd, ts], w_ffn[:, 2, kd, :]) for kd in range(KD)]).then_inc(fills(key), 1)
                    elif k == "pq":
                        _, h, m = key
                        pe.wait_ge(S["x2"], at(b, "x2", 2 * h + 2))
                        take(pe, b, key)
                        product(bank[plan[key][0][0]],
                                [(w_q1[:, kd, m * P:(m + 1) * P], x2T[:, kd, h * HALF:(h + 1) * HALF]) for kd in range(KD)])\
                            .then_inc(fills(key), 1)
                    elif k == "pk":
                        h = key[1]
                        take(pe, b, key)
                        product(bank[plan[key][0][0]][0:64, :],
                                [(w_vk1[:, kd, 64:128], x2T[:, kd, h * HALF:(h + 1) * HALF]) for kd in range(KD)]).then_inc(fills(key), 1)
                    elif k == "pv":
                        h = key[1]
                        take(pe, b, key)
                        for t in range(TT):
                            last = product(bank[plan[key][0][0]][:, t * P:(t + 1) * P],
                                           [(x2T[:, kd, (h * TT + t) * P:(h * TT + t + 1) * P], w_vk1[:, kd, :]) for kd in range(KD)])
                        last.then_inc(fills(key), 1)
                    elif k == "mx":
                        _, g, n, j = key
                        h, t = n // NT, n % NT
                        if (n, j) == (0, 0):
                            if g == 0:
                                pe.wait_ge(S["ks"], at(b, "ks", 96))
                            pe.wait_ge(S[f"qs{g % 3}"], at(b, f"qs{g % 3}", 96 * (g // 3 + 1)))
                        take(pe, b, key)
                        mm(bank[plan[key][0][0]], q_buf[g % 3][0:96, h, t * P:(t + 1) * P],
                           k_stack[0:96, g, j * HALF:(j + 1) * HALF], start=True, stop=True).then_inc(fills(key), 1)
                    elif k == "mt":
                        g = key[1]
                        pe.wait_ge(S["nm"], at(b, "nm", g + 1))
                        take(pe, b, key)
                        flip(key, [neg[:]])
                    elif k == "s":
                        _, g, c, h = key
                        if c == 0 and h == 0:
                            pe.wait_ge(S[f"m{g % 3}"], at(b, f"m{g % 3}", 48 * (g // 3 + 1)))
                        take(pe, b, key)
                        banks = plan[key][0]
                        for j in range(2):
                            last = mm(bank[banks[j]], k_stack[:, g, c * P:(c + 1) * P], q_buf[g % 3][:, h, j * HALF:(j + 1) * HALF],
                                      start=True, stop=True)
                        last.then_inc(fills(key), 1)
                    elif k == "av":
                        _, g, c, j = key
                        if c == 0 and j == 0:
                            take(pe, b, ("ot", g))
                            if g == 0:
                                pe.wait_ge(S["v1"], at(b, "v1", 2))
                        if j == 0:
                            pe.wait_ge(S["p"], at(b, "p", (g * NT + c + 1) * GR))
                        for h in range(GR):
                            last = mm(bank[6 + j][32 * h:32 * h + 32, :], v_aug[:, c, g, :],
                                      probs[:, 4 * (c % 2) + h, j * HALF:(j + 1) * HALF], start=(c == 0), stop=(c == NT - 1))
                        if (c, j) == (NT - 1, 1):
                            last.then_inc(fills(("ot", g)), 1)
                    elif k == "wo":
                        t = key[1]
                        if t % TT == 0:
                            pe.wait_ge(S["at"], at(b, "at", 2 * (t // TT) + 2))
                        take(pe, b, key)
                        product(bank[plan[key][0][0]][:, 0:D],
                                [(attn_T[:, kd, t * P:(t + 1) * P], w_o1[:, kd, :]) for kd in range(KD)]).then_inc(fills(key), 1)
                    elif k in ("h0", "h"):
                        _, h, f = key
                        whole = ("h", h, f)
                        if k == "h0":
                            if f == 0:
                                pe.wait_ge(S["x3"], at(b, "x3", 2 * h + 2))
                            take(pe, b, whole)
                        kd = int(k == "h")
                        last = mm(bank[plan[whole][0][0]], w_f1[:, kd, f * P:(f + 1) * P],
                                  x3T[:, kd, 1 + h * HALF:1 + (h + 1) * HALF], start=(kd == 0), stop=(kd == KD - 1))
                        if k == "h":
                            last.then_inc(fills(whole), 1)
                    elif k in ("w20", "w2p", "w2"):
                        _, h, t = key[:3]
                        whole = ("w2", h, t)
                        if k == "w20":
                            if t == 0:
                                pe.wait_ge(S["act"], at(b, "act", NF * (h + 1)))
                            take(pe, b, whole)
                        i = {"w20": 0, "w2": 3}[k] if k != "w2p" else key[3]
                        for f in (2 * i, 2 * i + 1):
                            last = mm(bank[plan[whole][0][0]][:, 0:D], hidden[:, h, f, t * P:(t + 1) * P], w_f2[:, f, :],
                                      start=(f == 0), stop=(f == NF - 1))
                        if k == "w2":
                            last.then_inc(fills(whole), 1)

            turn(Turn(0, "first"))
            with pe.Fori(1, NB) as i:
                turn(Turn(i, "loop"))
            turn(Turn(NB, "last"))


INPUTS = {
    "x": "L0_attn_x", "wq": "L0_attn_W_Q", "wk": "L0_attn_W_K", "wv": "L0_attn_W_V", "wg": "L0_attn_W_g_w",
    "gb": "L0_attn_W_g_b", "wo": "L0_attn_W_O", "dl": "L0_attn_decay_log", "fr": "L0_ffn_W_r", "fk": "L0_ffn_W_k",
    "fv": "L0_ffn_W_v", "mu_r": "L0_ffn_mu_r", "mu_k": "L0_ffn_mu_k", "Wq": "L1_attn_Wq", "bq": "L1_attn_bq",
    "Wk": "L1_attn_Wk", "bk": "L1_attn_bk", "Wv": "L1_attn_Wv", "bv": "L1_attn_bv", "Wo": "L1_attn_Wo",
    "bo": "L1_attn_bo", "W1": "L1_ffn_W1", "b1": "L1_ffn_b1", "ph": "L1_ffn_quantum_phases",
    "wr": "L1_ffn_quantum_weights_real", "wi": "L1_ffn_quantum_weights_imag", "W2": "L1_ffn_W2", "b2": "L1_ffn_b2",
}
TRANSPOSED = ("wq", "wk", "wv", "wg", "wo", "fr", "fk", "fv")


def kernel(**inputs):
    import concourse.bacc as bacc
    from concourse.bass_utils import run_bass_kernel_spmd

    nc = bacc.Bacc("TRN2", target_bir_lowering=False, num_devices=1,
                    dynamic_dma_scratch_size=1024)
    arrays, A = {}, {}
    for name, long in INPUTS.items():
        a = np.asarray(inputs[long])
        if name in TRANSPOSED:
            a = a.T
        a = np.ascontiguousarray(a)
        arrays[name] = a
        A[name] = nc.dram_tensor(name, a.shape, mybir.dt.from_np(a.dtype), kind="ExternalInput").ap()
    shape = arrays["x"].shape
    out = nc.dram_tensor("out", shape, F32, kind="ExternalOutput").ap()
    nc.disable_value_cache = True
    program(nc, A, out)
    r = run_bass_kernel_spmd(nc, [arrays], core_ids=[0])
    return r.results[0]["out"]
```
